# Optimizing a Trainium2 kernel written in Bass

```python
import numpy as np
import jax
import jax.numpy as jnp

def _softmax(x, axis=-1):
    return jax.nn.softmax(x, axis=axis)

def _gelu(x):
    return jax.nn.gelu(x, approximate=True)

def _silu(x):
    return jax.nn.silu(x)

def _sigmoid(x):
    return jax.nn.sigmoid(x)

def _layernorm(x, axis=-1, eps=1e-05):
    m = jnp.mean(x, axis=axis, keepdims=True)
    v = jnp.var(x, axis=axis, keepdims=True)
    return (x - m) / jnp.sqrt(v + eps)

def _scatter_add(tgt, idx, src, axis=0):
    return tgt.at[idx].add(src)

def _segment_sum(src, seg, n):
    return jax.ops.segment_sum(src, seg, n)
kernel_name = 'mk_decoder_postln_d2_seqx_r8_2d2056'

def setup_inputs(seed: int=0):
    np.random.seed(seed)
    _w = jnp.asarray

    def _rec_inputs():
        import jax
        import jax.numpy as jnp
        _rk = jax.random.key(seed)
        x = 7.22e-05 + 1 * jax.random.normal(jax.random.fold_in(_rk, 1), (2, 512, 128), jnp.float32)
        _lenS = 512 - jax.random.randint(jax.random.fold_in(_rk, 7), (2,), 0, max(1, 512 // 4) + 1, jnp.int32)
        _lenS2 = 77 - jax.random.randint(jax.random.fold_in(_rk, 8), (2,), 0, max(1, 77 // 4) + 1, jnp.int32)
        _ctx_768P = jax.random.normal(jax.random.fold_in(_rk, 11), (2, 16, 96), jnp.float32)
        _ctx_768c = jax.random.dirichlet(jax.random.fold_in(_rk, 511), 0.3 * jnp.ones((16,), jnp.float32), (2, 77))
        _ctx_768t = jnp.einsum('bsk,bkd->bsd', _ctx_768c, _ctx_768P)
        _ctx_768t = _ctx_768t * jax.lax.rsqrt(jnp.mean(jnp.square(_ctx_768t)) + 1e-12) * 0.953939
        ctx_768 = 3.88148e-05 + 0.999967 * (_ctx_768t + 0.3 * jax.random.normal(jax.random.fold_in(_rk, 611), (2, 77, 96), jnp.float32))
        _validS = jnp.arange(512)[None, :] < _lenS[:, None]
        _validS2 = jnp.arange(77)[None, :] < _lenS2[:, None]
        _causal = jnp.tril(jnp.ones((512, 512), dtype=bool))
        mask_BxS_bf1 = jnp.ones((2, 512), dtype=bool)
        mask_BxS2_bf1 = jnp.ones((2, 77), dtype=bool)
        return (x, ctx_768, mask_BxS_bf1, mask_BxS2_bf1)
    x, ctx_768, mask_BxS_bf1, mask_BxS2_bf1 = _rec_inputs()

    def _L0_attn_setup():
        import jax, jax.numpy as jnp
        import numpy as np
        N_HEAD = 16
        EPS = 1e-06

        def _linear_attention(q, k, v):
            B, H, D = (q.shape[1], q.shape[2], q.shape[3])

            def step(carry, qkv_t):
                S, z = carry
                qt, kt, vt = qkv_t
                S = S + kt[..., :, None] * vt[..., None, :]
                z = z + kt
                num = jnp.einsum('bhi,bhij->bhj', qt, S)
                den = jnp.sum(qt * z, axis=-1, keepdims=True)
                return ((S, z), num / (den + EPS))
            S0 = jnp.zeros((B, H, D, D), q.dtype)
            z0 = jnp.zeros((B, H, D), q.dtype)
            _, y = jax.lax.scan(step, (S0, z0), (q, k, v))
            return y
        key = jax.random.key(seed)
        k1, k2, k3 = jax.random.split(key, 3)
        B, T, C = (2, 256, 128)
        x = jax.random.normal(k1, (B, T, C), dtype=jnp.float32)
        w_attn = jax.random.normal(k2, (C, 3 * C), dtype=jnp.float32) * 0.02
        w_proj = jax.random.normal(k3, (C, C), dtype=jnp.float32) * 0.02
        return {'x': x, 'w_attn': w_attn, 'w_proj': w_proj}
    _L0_attn_all = _L0_attn_setup()
    _L0_attn_in = {k: v for k, v in _L0_attn_all.items() if k in ('w_attn', 'w_proj')}
    del _L0_attn_all

    def _L0_xattn_setup():
        import jax, jax.numpy as jnp
        import numpy as np
        B, T, DT, G, DV = (16, 64, 128, 72, 96)
        H, DH = (4, 32)
        INNER = H * DH
        HID = 4 * DT
        N_STATE = 64
        K_TOP = 32

        def layernorm(x, g, b, eps=1e-05):
            m = x.mean(-1, keepdims=True)
            v = x.var(-1, keepdims=True)
            return (x - m) * jax.lax.rsqrt(v + eps) * g + b

        def s4d(x, log_dt, A_re, A_im, C_re, C_im, D_skip):
            Bb, L, D = x.shape
            dt = jnp.exp(log_dt)
            A = A_re + 1j * A_im
            C = C_re + 1j * C_im
            dtA = dt[:, None] * A
            dC = C * (jnp.exp(dtA) - 1.0) / A
            powers = jnp.exp(dtA[:, :, None] * jnp.arange(L))
            K = 2.0 * jnp.einsum('dn,dnl->dl', dC, powers).real
            n = 2 * L
            Kf = jnp.fft.rfft(K, n=n, axis=-1)
            xf = jnp.fft.rfft(x, n=n, axis=1)
            y = jnp.fft.irfft(xf * Kf.T[None], n=n, axis=1)[:, :L]
            return y + x * D_skip
        key = jax.random.key(seed)
        ks = jax.random.split(key, 16)
        s = 0.02
        inp = {'x_text': jax.random.normal(ks[0], (B, T, DT), jnp.float32), 'x_vision': jax.random.normal(ks[1], (B, G, DV), jnp.float32), 'text_mask': jnp.ones((B, T), bool), 'vision_mask': jnp.ones((B, G), bool), 'Wq': jax.random.normal(ks[2], (DT, INNER), jnp.float32) * s, 'Wk': jax.random.normal(ks[3], (DV, INNER), jnp.float32) * s, 'Wv': jax.random.normal(ks[4], (DV, DT), jnp.float32) * s, 'W_film_in': jax.random.normal(ks[5], (DT, 2 * DT), jnp.float32) * s, 'b_film_in': jnp.zeros((2 * DT,), jnp.float32), 'W_film_out': jax.random.normal(ks[6], (DT, 2 * DT), jnp.float32) * s, 'b_film_out': jnp.zeros((2 * DT,), jnp.float32), 'g_norm_in': jnp.ones((DT,), jnp.float32), 'b_norm_in': jnp.zeros((DT,), jnp.float32), 'g_norm_out': jnp.ones((DT,), jnp.float32), 'b_norm_out': jnp.zeros((DT,), jnp.float32), 'g_ffn': jnp.ones((DT,), jnp.float32), 'b_ffn': jnp.zeros((DT,), jnp.float32), 'W1': jax.random.normal(ks[7], (DT, HID), jnp.float32) * s, 'b1': jnp.zeros((HID,), jnp.float32), 'W2': jax.random.normal(ks[8], (HID, DT), jnp.float32) * s, 'b2': jnp.zeros((DT,), jnp.float32), 'log_dt': jnp.log(0.001) + jax.random.uniform(ks[9], (DT,), jnp.float32) * (jnp.log(0.1) - jnp.log(0.001)), 'A_re': -0.5 * jnp.ones((DT, N_STATE), jnp.float32), 'A_im': jnp.tile(jnp.pi * jnp.arange(N_STATE, dtype=jnp.float32), (DT, 1)), 'C_re': jax.random.normal(ks[10], (DT, N_STATE), jnp.float32) * 0.5 ** 0.5, 'C_im': jax.random.normal(ks[11], (DT, N_STATE), jnp.float32) * 0.5 ** 0.5, 'D_skip': jax.random.normal(ks[12], (DT,), jnp.float32), 'mod_gate': jnp.array(0.5, jnp.float32)}
        return inp
    _L0_xattn_all = _L0_xattn_setup()
    _L0_xattn_in = {k: v for k, v in _L0_xattn_all.items() if k in ('Wq', 'Wk', 'Wv', 'W_film_in', 'b_film_in', 'W_film_out', 'b_film_out', 'g_norm_in', 'b_norm_in', 'g_norm_out', 'b_norm_out', 'g_ffn', 'b_ffn', 'W1', 'b1', 'W2', 'b2', 'log_dt', 'A_re', 'A_im', 'C_re', 'C_im', 'D_skip', 'mod_gate')}
    del _L0_xattn_all

    def _L0_ffn_setup():
        import jax, jax.numpy as jnp
        import numpy as np
        HIDDEN = 128
        HEAD_DIM = 64
        N_EXPERTS = 16
        MIN_EXPERTS = 2
        B, T = (4, 256)

        def _normalize(x, axis):
            n = jnp.sqrt(jnp.sum(x * x, axis=axis, keepdims=True))
            return x / jnp.maximum(n, 1e-12)

        def _ste(x):
            hard = jax.lax.stop_gradient((x > 0).astype(x.dtype))
            return hard + x - jax.lax.stop_gradient(x)

        def _gating(hidden_states, sim_matrix, gates):
            b, t, c = hidden_states.shape
            flat = hidden_states.reshape(b * t, c)
            logits = _normalize(flat, -1) @ _normalize(sim_matrix, 0) - jax.nn.sigmoid(gates)
            gated = jax.nn.relu(logits)
            mask = _ste(gated)
            inactive = jnp.sum(mask, axis=1) == 0
            _, fb_idx = jax.lax.top_k(logits, MIN_EXPERTS)
            fb = jnp.zeros_like(mask).at[jnp.arange(b * t)[:, None], fb_idx].set(1.0)
            fb_applied = inactive[:, None] & (fb > 0)
            mask = jnp.where(fb_applied, 1.0, mask)
            masked_logits = jnp.where(mask > 0, gated, -jnp.inf)
            return jax.nn.softmax(masked_logits, axis=-1).reshape(b, t, -1)
        key = jax.random.key(seed)
        ks = jax.random.split(key, 6)
        xav_qkv = float(np.sqrt(6.0 / (HIDDEN + HEAD_DIM)))
        return {'hidden_states': jax.random.normal(ks[0], (B, T, HIDDEN), dtype=jnp.float32), 'sim_matrix': jax.random.normal(ks[1], (HIDDEN, N_EXPERTS), dtype=jnp.float32), 'gates': jnp.zeros((N_EXPERTS,), dtype=jnp.float32), 'q_proj': jax.random.uniform(ks[2], (N_EXPERTS, HIDDEN, HEAD_DIM), jnp.float32, -xav_qkv, xav_qkv), 'k_proj': jax.random.uniform(ks[3], (N_EXPERTS, HIDDEN, HEAD_DIM), jnp.float32, -xav_qkv, xav_qkv), 'v_proj': jax.random.uniform(ks[4], (N_EXPERTS, HIDDEN, HEAD_DIM), jnp.float32, -xav_qkv, xav_qkv), 'o_proj': jax.random.uniform(ks[5], (N_EXPERTS, HEAD_DIM, HIDDEN), jnp.float32, -xav_qkv, xav_qkv)}
    _L0_ffn_all = _L0_ffn_setup()
    _L0_ffn_in = {k: v for k, v in _L0_ffn_all.items() if k in ('sim_matrix', 'gates', 'q_proj', 'k_proj', 'v_proj', 'o_proj')}
    del _L0_ffn_all

    def _L1_attn_setup():
        import jax, jax.numpy as jnp
        import numpy as np
        B, T, D = (8, 256, 128)
        H, C, DV = (8, 64, 128)
        LN_EPS = 1e-05
        NORM_EPS = 1e-12

        def _xavier(k, shape, fan_in, fan_out):
            lim = float(np.sqrt(6.0 / (fan_in + fan_out)))
            return jax.random.uniform(k, shape, jnp.float32, -lim, lim)

        def _forward(x, Wq, Wk, Wv, Qc, Vc, Wa_w, Wa_b, Wo, gamma, beta):
            residual = x
            mu = jnp.mean(x, axis=-1, keepdims=True)
            var = jnp.mean(jnp.square(x - mu), axis=-1, keepdims=True)
            xn = (x - mu) * jax.lax.rsqrt(var + LN_EPS) * gamma + beta
            q_lat = xn @ Wq.T
            k_lat = xn @ Wk.T
            v_lat = xn @ Wv.T
            q = jnp.einsum('btc,hce->bhte', q_lat, Qc)
            v = jnp.einsum('btc,hcd->bhtd', v_lat, Vc)
            alpha = jax.nn.sigmoid(xn @ Wa_w.T + Wa_b)
            alpha = alpha.reshape(x.shape[0], x.shape[1], H, C).transpose(0, 2, 1, 3)
            kn = k_lat / jnp.maximum(jnp.linalg.norm(k_lat, axis=-1, keepdims=True), NORM_EPS)
            qs = jnp.moveaxis(q, 2, 0)
            vs = jnp.moveaxis(v, 2, 0)
            als = jnp.moveaxis(alpha, 2, 0)
            kns = jnp.moveaxis(kn, 1, 0)
            S0 = jnp.zeros((x.shape[0], H, C, DV), x.dtype)

            def step(S, inp):
                q_t, k_t, v_t, a_t = inp
                S = a_t[..., None] * S + k_t[:, None, :, None] * v_t[..., None, :]
                o_t = jnp.einsum('bhcv,bhc->bhv', S, q_t)
                return (S, o_t)
            _, outs = jax.lax.scan(step, S0, (qs, kns, vs, als))
            out = jnp.moveaxis(outs, 0, 1).reshape(x.shape[0], x.shape[1], H * DV)
            return out @ Wo.T + residual
        key = jax.random.key(seed)
        ks = jax.random.split(key, 9)
        x = jax.random.normal(ks[0], (B, T, D), jnp.float32)
        Wq = _xavier(ks[1], (C, D), D, C)
        Wk = _xavier(ks[2], (C, D), D, C)
        Wv = _xavier(ks[3], (C, D), D, C)
        Qc = _xavier(ks[4], (H, C, C), C, C)
        Vc = _xavier(ks[5], (H, C, DV), C, DV)
        Wa_w = _xavier(ks[6], (H * C, D), D, H * C)
        Wa_b = jnp.full((H * C,), 3.0, jnp.float32)
        Wo = _xavier(ks[7], (D, H * DV), H * DV, D)
        gamma = jnp.ones((D,), jnp.float32)
        beta = jnp.zeros((D,), jnp.float32)
        return {'x': x, 'Wq': Wq, 'Wk': Wk, 'Wv': Wv, 'Qc': Qc, 'Vc': Vc, 'Wa_w': Wa_w, 'Wa_b': Wa_b, 'Wo': Wo, 'gamma': gamma, 'beta': beta}
    _L1_attn_all = _L1_attn_setup()
    _L1_attn_in = {k: v for k, v in _L1_attn_all.items() if k in ('Wq', 'Wk', 'Wv', 'Qc', 'Vc', 'Wa_w', 'Wa_b', 'Wo', 'gamma', 'beta')}
    del _L1_attn_all

    def _L1_xattn_setup():
        import jax, jax.numpy as jnp
        import numpy as np
        NUM_HEADS = 16
        CLAMP = 10000.0
        key = jax.random.key(seed)
        ks = jax.random.split(key, 8)
        B, Nq, Nkv, Cq, Ckv = (4, 256, 256, 128, 96)
        s_q = 1.0 / np.sqrt(Cq)
        s_kv = 1.0 / np.sqrt(Ckv)
        return {'query': jax.random.normal(ks[0], (B, Nq, Cq), jnp.float32), 'key_value': jax.random.normal(ks[1], (B, Nkv, Ckv), jnp.float32), 'Wq': jax.random.normal(ks[2], (Cq, Cq), jnp.float32) * s_q, 'bq': jnp.zeros((Cq,), jnp.float32), 'Wk': jax.random.normal(ks[3], (Ckv, Cq), jnp.float32) * s_kv, 'bk': jnp.zeros((Cq,), jnp.float32), 'Wv': jax.random.normal(ks[4], (Ckv, Cq), jnp.float32) * s_kv, 'bv': jnp.zeros((Cq,), jnp.float32), 'Wo': jax.random.normal(ks[5], (Cq, Cq), jnp.float32) * s_q, 'bo': jnp.zeros((Cq,), jnp.float32)}
    _L1_xattn_all = _L1_xattn_setup()
    _L1_xattn_in = {k: v for k, v in _L1_xattn_all.items() if k in ('Wq', 'bq', 'Wk', 'bk', 'Wv', 'bv', 'Wo', 'bo')}
    del _L1_xattn_all

    def _L1_ffn_setup():
        import jax, jax.numpy as jnp
        import numpy as np
        B, T, D = (2, 128, 128)
        E = 16
        H = 256
        K = 2
        HS = H * 2
        key = jax.random.key(seed)
        ks = jax.random.split(key, 16)
        s = 0.02
        f32 = jnp.float32
        return {'x': jax.random.normal(ks[0], (B, T, D), f32), 'Wg': jax.random.normal(ks[1], (D, E), f32) * s, 'W1': jax.random.normal(ks[2], (E, D, H), f32) * s, 'b1': jax.random.normal(ks[3], (E, H), f32) * s, 'W11': jax.random.normal(ks[4], (E, D, H), f32) * s, 'b11': jax.random.normal(ks[5], (E, H), f32) * s, 'W2': jax.random.normal(ks[6], (E, H, D), f32) * s, 'b2': jax.random.normal(ks[7], (E, D), f32) * s, 'Ws1': jax.random.normal(ks[8], (D, HS), f32) * s, 'bs1': jax.random.normal(ks[9], (HS,), f32) * s, 'Ws11': jax.random.normal(ks[10], (D, HS), f32) * s, 'bs11': jax.random.normal(ks[11], (HS,), f32) * s, 'Ws2': jax.random.normal(ks[12], (HS, D), f32) * s, 'bs2': jax.random.normal(ks[13], (D,), f32) * s}
    _L1_ffn_all = _L1_ffn_setup()
    _L1_ffn_in = {k: v for k, v in _L1_ffn_all.items() if k in ('Wg', 'W1', 'b1', 'W11', 'b11', 'W2', 'b2', 'Ws1', 'bs1', 'Ws11', 'bs11', 'Ws2', 'bs2')}
    del _L1_ffn_all
    return {'x': x, 'ctx_768': ctx_768, 'mask_BxS_bf1': mask_BxS_bf1, 'mask_BxS2_bf1': mask_BxS2_bf1, 'L0_attn_w_attn': _L0_attn_in['w_attn'], 'L0_attn_w_proj': _L0_attn_in['w_proj'], 'L0_xattn_Wq': _L0_xattn_in['Wq'], 'L0_xattn_Wk': _L0_xattn_in['Wk'], 'L0_xattn_Wv': _L0_xattn_in['Wv'], 'L0_xattn_W_film_in': _L0_xattn_in['W_film_in'], 'L0_xattn_b_film_in': _L0_xattn_in['b_film_in'], 'L0_xattn_W_film_out': _L0_xattn_in['W_film_out'], 'L0_xattn_b_film_out': _L0_xattn_in['b_film_out'], 'L0_xattn_g_norm_in': _L0_xattn_in['g_norm_in'], 'L0_xattn_b_norm_in': _L0_xattn_in['b_norm_in'], 'L0_xattn_g_norm_out': _L0_xattn_in['g_norm_out'], 'L0_xattn_b_norm_out': _L0_xattn_in['b_norm_out'], 'L0_xattn_g_ffn': _L0_xattn_in['g_ffn'], 'L0_xattn_b_ffn': _L0_xattn_in['b_ffn'], 'L0_xattn_W1': _L0_xattn_in['W1'], 'L0_xattn_b1': _L0_xattn_in['b1'], 'L0_xattn_W2': _L0_xattn_in['W2'], 'L0_xattn_b2': _L0_xattn_in['b2'], 'L0_xattn_log_dt': _L0_xattn_in['log_dt'], 'L0_xattn_A_re': _L0_xattn_in['A_re'], 'L0_xattn_A_im': _L0_xattn_in['A_im'], 'L0_xattn_C_re': _L0_xattn_in['C_re'], 'L0_xattn_C_im': _L0_xattn_in['C_im'], 'L0_xattn_D_skip': _L0_xattn_in['D_skip'], 'L0_xattn_mod_gate': _L0_xattn_in['mod_gate'], 'L0_ffn_sim_matrix': _L0_ffn_in['sim_matrix'], 'L0_ffn_gates': _L0_ffn_in['gates'], 'L0_ffn_q_proj': _L0_ffn_in['q_proj'], 'L0_ffn_k_proj': _L0_ffn_in['k_proj'], 'L0_ffn_v_proj': _L0_ffn_in['v_proj'], 'L0_ffn_o_proj': _L0_ffn_in['o_proj'], 'L1_attn_Wq': _L1_attn_in['Wq'], 'L1_attn_Wk': _L1_attn_in['Wk'], 'L1_attn_Wv': _L1_attn_in['Wv'], 'L1_attn_Qc': _L1_attn_in['Qc'], 'L1_attn_Vc': _L1_attn_in['Vc'], 'L1_attn_Wa_w': _L1_attn_in['Wa_w'], 'L1_attn_Wa_b': _L1_attn_in['Wa_b'], 'L1_attn_Wo': _L1_attn_in['Wo'], 'L1_attn_gamma': _L1_attn_in['gamma'], 'L1_attn_beta': _L1_attn_in['beta'], 'L1_xattn_Wq': _L1_xattn_in['Wq'], 'L1_xattn_bq': _L1_xattn_in['bq'], 'L1_xattn_Wk': _L1_xattn_in['Wk'], 'L1_xattn_bk': _L1_xattn_in['bk'], 'L1_xattn_Wv': _L1_xattn_in['Wv'], 'L1_xattn_bv': _L1_xattn_in['bv'], 'L1_xattn_Wo': _L1_xattn_in['Wo'], 'L1_xattn_bo': _L1_xattn_in['bo'], 'L1_ffn_Wg': _L1_ffn_in['Wg'], 'L1_ffn_W1': _L1_ffn_in['W1'], 'L1_ffn_b1': _L1_ffn_in['b1'], 'L1_ffn_W11': _L1_ffn_in['W11'], 'L1_ffn_b11': _L1_ffn_in['b11'], 'L1_ffn_W2': _L1_ffn_in['W2'], 'L1_ffn_b2': _L1_ffn_in['b2'], 'L1_ffn_Ws1': _L1_ffn_in['Ws1'], 'L1_ffn_bs1': _L1_ffn_in['bs1'], 'L1_ffn_Ws11': _L1_ffn_in['Ws11'], 'L1_ffn_bs11': _L1_ffn_in['bs11'], 'L1_ffn_Ws2': _L1_ffn_in['Ws2'], 'L1_ffn_bs2': _L1_ffn_in['bs2']}

def reference(x, ctx_768, mask_BxS_bf1, mask_BxS2_bf1, L0_attn_w_attn, L0_attn_w_proj, L0_xattn_Wq, L0_xattn_Wk, L0_xattn_Wv, L0_xattn_W_film_in, L0_xattn_b_film_in, L0_xattn_W_film_out, L0_xattn_b_film_out, L0_xattn_g_norm_in, L0_xattn_b_norm_in, L0_xattn_g_norm_out, L0_xattn_b_norm_out, L0_xattn_g_ffn, L0_xattn_b_ffn, L0_xattn_W1, L0_xattn_b1, L0_xattn_W2, L0_xattn_b2, L0_xattn_log_dt, L0_xattn_A_re, L0_xattn_A_im, L0_xattn_C_re, L0_xattn_C_im, L0_xattn_D_skip, L0_xattn_mod_gate, L0_ffn_sim_matrix, L0_ffn_gates, L0_ffn_q_proj, L0_ffn_k_proj, L0_ffn_v_proj, L0_ffn_o_proj, L1_attn_Wq, L1_attn_Wk, L1_attn_Wv, L1_attn_Qc, L1_attn_Vc, L1_attn_Wa_w, L1_attn_Wa_b, L1_attn_Wo, L1_attn_gamma, L1_attn_beta, L1_xattn_Wq, L1_xattn_bq, L1_xattn_Wk, L1_xattn_bk, L1_xattn_Wv, L1_xattn_bv, L1_xattn_Wo, L1_xattn_bo, L1_ffn_Wg, L1_ffn_W1, L1_ffn_b1, L1_ffn_W11, L1_ffn_b11, L1_ffn_W2, L1_ffn_b2, L1_ffn_Ws1, L1_ffn_bs1, L1_ffn_Ws11, L1_ffn_bs11, L1_ffn_Ws2, L1_ffn_bs2):
    import jax
    import jax.numpy as jnp

    def _L0_attn_ref(x, w_attn, w_proj):
        import jax, jax.numpy as jnp
        import numpy as np
        N_HEAD = 16
        EPS = 1e-06

        def _linear_attention(q, k, v):
            B, H, D = (q.shape[1], q.shape[2], q.shape[3])

            def step(carry, qkv_t):
                S, z = carry
                qt, kt, vt = qkv_t
                S = S + kt[..., :, None] * vt[..., None, :]
                z = z + kt
                num = jnp.einsum('bhi,bhij->bhj', qt, S)
                den = jnp.sum(qt * z, axis=-1, keepdims=True)
                return ((S, z), num / (den + EPS))
            S0 = jnp.zeros((B, H, D, D), q.dtype)
            z0 = jnp.zeros((B, H, D), q.dtype)
            _, y = jax.lax.scan(step, (S0, z0), (q, k, v))
            return y
        B, T, C = x.shape
        H = N_HEAD
        D = C // H
        qkv = x @ w_attn
        q, k, v = jnp.split(qkv, 3, axis=-1)

        def to_tbhd(a):
            return a.reshape(B, T, H, D).transpose(1, 0, 2, 3)
        q = jax.nn.elu(to_tbhd(q)) + 1.0
        k = jax.nn.elu(to_tbhd(k)) + 1.0
        v = to_tbhd(v)
        y = _linear_attention(q, k, v)
        y = y.transpose(1, 0, 2, 3).reshape(B, T, C)
        return y @ w_proj

    def _L0_xattn_ref(x_text, x_vision, text_mask, vision_mask, Wq, Wk, Wv, W_film_in, b_film_in, W_film_out, b_film_out, g_norm_in, b_norm_in, g_norm_out, b_norm_out, g_ffn, b_ffn, W1, b1, W2, b2, log_dt, A_re, A_im, C_re, C_im, D_skip, mod_gate):
        import jax, jax.numpy as jnp
        import numpy as np
        B, T, DT, G, DV = (16, 64, 128, 72, 96)
        H, DH = (4, 32)
        INNER = H * DH
        HID = 4 * DT
        N_STATE = 64
        K_TOP = 32

        def layernorm(x, g, b, eps=1e-05):
            m = x.mean(-1, keepdims=True)
            v = x.var(-1, keepdims=True)
            return (x - m) * jax.lax.rsqrt(v + eps) * g + b

        def s4d(x, log_dt, A_re, A_im, C_re, C_im, D_skip):
            Bb, L, D = x.shape
            dt = jnp.exp(log_dt)
            A = A_re + 1j * A_im
            C = C_re + 1j * C_im
            dtA = dt[:, None] * A
            dC = C * (jnp.exp(dtA) - 1.0) / A
            powers = jnp.exp(dtA[:, :, None] * jnp.arange(L))
            K = 2.0 * jnp.einsum('dn,dnl->dl', dC, powers).real
            n = 2 * L
            Kf = jnp.fft.rfft(K, n=n, axis=-1)
            xf = jnp.fft.rfft(x, n=n, axis=1)
            y = jnp.fft.irfft(xf * Kf.T[None], n=n, axis=1)[:, :L]
            return y + x * D_skip
        Bb, Tt, D = x_text.shape
        Gg = x_vision.shape[1]
        Q = (x_text @ Wq).reshape(Bb, Tt, H, DH)
        K = (x_vision @ Wk).reshape(Bb, Gg, H, DH)
        scores = jnp.einsum('bthd,bghd->bhtg', Q, K) / np.sqrt(DH).astype(np.float32)
        scores = jnp.where(vision_mask[:, None, None, :], scores, -jnp.inf)
        topv, topi = jax.lax.top_k(scores, K_TOP)
        probs = jax.nn.softmax(topv, axis=-1)
        bi = jnp.arange(Bb)[:, None, None, None]
        hi = jnp.arange(H)[None, :, None, None]
        ti = jnp.arange(Tt)[None, None, :, None]
        attn = jnp.zeros_like(scores).at[bi, hi, ti, topi].set(probs)
        attn_mean = attn.mean(axis=1)
        V = x_vision @ Wv
        c_t = jnp.einsum('btg,bgd->btd', attn_mean, V)
        c_t = c_t * text_mask[..., None]
        x = layernorm(x_text, g_norm_in, b_norm_in)
        scale_in, shift_in = jnp.split(c_t @ W_film_in + b_film_in, 2, axis=-1)
        x = x * (1.0 + mod_gate * scale_in) + mod_gate * shift_in
        y = s4d(x, log_dt, A_re, A_im, C_re, C_im, D_skip)
        scale_out, shift_out = jnp.split(c_t @ W_film_out + b_film_out, 2, axis=-1)
        y = y * (1.0 + mod_gate * scale_out) + mod_gate * shift_out
        xt = x_text + y
        h = layernorm(xt, g_ffn, b_ffn)
        h = jax.nn.gelu(h @ W1 + b1, approximate=False) @ W2 + b2
        xt = xt + h
        return layernorm(xt, g_norm_out, b_norm_out)

    def _L0_ffn_ref(hidden_states, sim_matrix, gates, q_proj, k_proj, v_proj, o_proj):
        import jax, jax.numpy as jnp
        import numpy as np
        HIDDEN = 128
        HEAD_DIM = 64
        N_EXPERTS = 16
        MIN_EXPERTS = 2
        B, T = (4, 256)

        def _normalize(x, axis):
            n = jnp.sqrt(jnp.sum(x * x, axis=axis, keepdims=True))
            return x / jnp.maximum(n, 1e-12)

        def _ste(x):
            hard = jax.lax.stop_gradient((x > 0).astype(x.dtype))
            return hard + x - jax.lax.stop_gradient(x)

        def _gating(hidden_states, sim_matrix, gates):
            b, t, c = hidden_states.shape
            flat = hidden_states.reshape(b * t, c)
            logits = _normalize(flat, -1) @ _normalize(sim_matrix, 0) - jax.nn.sigmoid(gates)
            gated = jax.nn.relu(logits)
            mask = _ste(gated)
            inactive = jnp.sum(mask, axis=1) == 0
            _, fb_idx = jax.lax.top_k(logits, MIN_EXPERTS)
            fb = jnp.zeros_like(mask).at[jnp.arange(b * t)[:, None], fb_idx].set(1.0)
            fb_applied = inactive[:, None] & (fb > 0)
            mask = jnp.where(fb_applied, 1.0, mask)
            masked_logits = jnp.where(mask > 0, gated, -jnp.inf)
            return jax.nn.softmax(masked_logits, axis=-1).reshape(b, t, -1)
        b, t, c = hidden_states.shape
        rw = _gating(hidden_states, sim_matrix, gates)
        q = jnp.einsum('bte,bted->btd', rw, jnp.einsum('btc,ecd->bted', hidden_states, q_proj))
        k = jnp.einsum('bte,bted->btd', rw, jnp.einsum('btc,ecd->bted', hidden_states, k_proj))
        v = jnp.einsum('bte,bted->btd', rw, jnp.einsum('btc,ecd->bted', hidden_states, v_proj))
        scale = 1.0 / jnp.sqrt(jnp.asarray(HEAD_DIM, dtype=q.dtype))
        scores = jnp.einsum('bqd,bkd->bqk', q, k) * scale
        causal = jnp.tril(jnp.ones((t, t), dtype=bool))
        scores = jnp.where(causal, scores, -jnp.inf)
        attn = jnp.einsum('bqk,bkd->bqd', jax.nn.softmax(scores, axis=-1), v)
        mixed = attn[:, :, None, :] * rw[..., None]
        return jnp.einsum('bted,edc->btc', mixed, o_proj)

    def _L1_attn_ref(x, Wq, Wk, Wv, Qc, Vc, Wa_w, Wa_b, Wo, gamma, beta):
        import jax, jax.numpy as jnp
        import numpy as np
        B, T, D = (8, 256, 128)
        H, C, DV = (8, 64, 128)
        LN_EPS = 1e-05
        NORM_EPS = 1e-12

        def _xavier(k, shape, fan_in, fan_out):
            lim = float(np.sqrt(6.0 / (fan_in + fan_out)))
            return jax.random.uniform(k, shape, jnp.float32, -lim, lim)

        def _forward(x, Wq, Wk, Wv, Qc, Vc, Wa_w, Wa_b, Wo, gamma, beta):
            residual = x
            mu = jnp.mean(x, axis=-1, keepdims=True)
            var = jnp.mean(jnp.square(x - mu), axis=-1, keepdims=True)
            xn = (x - mu) * jax.lax.rsqrt(var + LN_EPS) * gamma + beta
            q_lat = xn @ Wq.T
            k_lat = xn @ Wk.T
            v_lat = xn @ Wv.T
            q = jnp.einsum('btc,hce->bhte', q_lat, Qc)
            v = jnp.einsum('btc,hcd->bhtd', v_lat, Vc)
            alpha = jax.nn.sigmoid(xn @ Wa_w.T + Wa_b)
            alpha = alpha.reshape(x.shape[0], x.shape[1], H, C).transpose(0, 2, 1, 3)
            kn = k_lat / jnp.maximum(jnp.linalg.norm(k_lat, axis=-1, keepdims=True), NORM_EPS)
            qs = jnp.moveaxis(q, 2, 0)
            vs = jnp.moveaxis(v, 2, 0)
            als = jnp.moveaxis(alpha, 2, 0)
            kns = jnp.moveaxis(kn, 1, 0)
            S0 = jnp.zeros((x.shape[0], H, C, DV), x.dtype)

            def step(S, inp):
                q_t, k_t, v_t, a_t = inp
                S = a_t[..., None] * S + k_t[:, None, :, None] * v_t[..., None, :]
                o_t = jnp.einsum('bhcv,bhc->bhv', S, q_t)
                return (S, o_t)
            _, outs = jax.lax.scan(step, S0, (qs, kns, vs, als))
            out = jnp.moveaxis(outs, 0, 1).reshape(x.shape[0], x.shape[1], H * DV)
            return out @ Wo.T + residual
        return _forward(x, Wq, Wk, Wv, Qc, Vc, Wa_w, Wa_b, Wo, gamma, beta)

    def _L1_xattn_ref(query, key_value, Wq, bq, Wk, bk, Wv, bv, Wo, bo):
        import jax, jax.numpy as jnp
        import numpy as np
        NUM_HEADS = 16
        CLAMP = 10000.0
        B, Nq, Cq = query.shape
        Nkv = key_value.shape[1]
        H = NUM_HEADS
        D = Cq // H
        scale = D ** (-0.5)
        q = (query @ Wq + bq).reshape(B, Nq, H, D).transpose(0, 2, 1, 3)
        k = (key_value @ Wk + bk).reshape(B, Nkv, H, D).transpose(0, 2, 1, 3)
        v = (key_value @ Wv + bv).reshape(B, Nkv, H, D).transpose(0, 2, 1, 3)
        attn = jnp.einsum('bhqd,bhkd->bhqk', q, k) * scale
        attn = jnp.clip(attn, -CLAMP, CLAMP)
        attn = jax.nn.softmax(attn, axis=-1)
        attn = jnp.where(jnp.any(jnp.isnan(attn)), jnp.asarray(1.0 / Nkv, attn.dtype), attn)
        x = jnp.einsum('bhqk,bhkd->bqhd', attn, v).reshape(B, Nq, Cq)
        return x @ Wo + bo

    def _L1_ffn_ref(x, Wg, W1, b1, W11, b11, W2, b2, Ws1, bs1, Ws11, bs11, Ws2, bs2):
        import jax, jax.numpy as jnp
        import numpy as np
        B, T, D = (2, 128, 128)
        E = 16
        H = 256
        K = 2
        HS = H * 2
        b, t, d = x.shape
        xf = x.reshape(b * t, d)
        n = xf.shape[0]
        logits = xf @ Wg
        _, topi = jax.lax.top_k(logits, K)
        mask = jnp.zeros((n, E), bool).at[jnp.arange(n)[:, None], topi].set(True)
        gates = jax.nn.softmax(jnp.where(mask, logits, -jnp.inf), axis=-1)
        y = jnp.zeros_like(xf)
        for e in range(E):
            h = jax.nn.silu(xf @ W1[e] + b1[e]) * (xf @ W11[e] + b11[e])
            y = y + (h @ W2[e] + b2[e]) * gates[:, e, None]
        z = jax.nn.silu(xf @ Ws1 + bs1) * (xf @ Ws11 + bs11) @ Ws2 + bs2
        return (y + z).reshape(b, t, d)
    x = _layernorm(x + _L0_attn_ref(x, L0_attn_w_attn, L0_attn_w_proj), axis=-1)
    x = _layernorm(x + _L0_xattn_ref(x, ctx_768, mask_BxS_bf1, mask_BxS2_bf1, L0_xattn_Wq, L0_xattn_Wk, L0_xattn_Wv, L0_xattn_W_film_in, L0_xattn_b_film_in, L0_xattn_W_film_out, L0_xattn_b_film_out, L0_xattn_g_norm_in, L0_xattn_b_norm_in, L0_xattn_g_norm_out, L0_xattn_b_norm_out, L0_xattn_g_ffn, L0_xattn_b_ffn, L0_xattn_W1, L0_xattn_b1, L0_xattn_W2, L0_xattn_b2, L0_xattn_log_dt, L0_xattn_A_re, L0_xattn_A_im, L0_xattn_C_re, L0_xattn_C_im, L0_xattn_D_skip, L0_xattn_mod_gate), axis=-1)
    x = _layernorm(x + _L0_ffn_ref(x, L0_ffn_sim_matrix, L0_ffn_gates, L0_ffn_q_proj, L0_ffn_k_proj, L0_ffn_v_proj, L0_ffn_o_proj), axis=-1)
    x = _layernorm(x + _L1_attn_ref(x, L1_attn_Wq, L1_attn_Wk, L1_attn_Wv, L1_attn_Qc, L1_attn_Vc, L1_attn_Wa_w, L1_attn_Wa_b, L1_attn_Wo, L1_attn_gamma, L1_attn_beta), axis=-1)
    x = _layernorm(x + _L1_xattn_ref(x, ctx_768, L1_xattn_Wq, L1_xattn_bq, L1_xattn_Wk, L1_xattn_bk, L1_xattn_Wv, L1_xattn_bv, L1_xattn_Wo, L1_xattn_bo), axis=-1)
    x = _layernorm(x + _L1_ffn_ref(x, L1_ffn_Wg, L1_ffn_W1, L1_ffn_b1, L1_ffn_W11, L1_ffn_b11, L1_ffn_W2, L1_ffn_b2, L1_ffn_Ws1, L1_ffn_bs1, L1_ffn_Ws11, L1_ffn_bs11, L1_ffn_Ws2, L1_ffn_bs2), axis=-1)
    return x

_drawn_inputs = setup_inputs


def setup_inputs(seed=0):
    import zlib

    import numpy as np

    out = dict(_drawn_inputs(seed))
    spreads = {'L0_xattn_b_film_in': (0.0, 0.1),
     'L0_xattn_b_film_out': (0.0, 0.1),
     'L0_xattn_g_norm_in': (1.0, 0.2),
     'L0_xattn_b_norm_in': (0.0, 0.1),
     'L0_xattn_g_norm_out': (1.0, 0.2),
     'L0_xattn_b_norm_out': (0.0, 0.1),
     'L0_xattn_g_ffn': (1.0, 0.6),
     'L0_xattn_b_ffn': (0.0, 0.8),
     'L0_xattn_b1': (0.0, 0.287),
     'L0_xattn_b2': (0.0, 0.1),
     'L0_xattn_A_re': (-0.5, 0.2),
     'L0_ffn_gates': (0.0, 0.1),
     'L1_attn_Wa_b': (3.0, 0.2),
     'L1_attn_gamma': (1.0, 0.2),
     'L1_attn_beta': (0.0, 0.1),
     'L1_xattn_bq': (0.0, 0.397),
     'L1_xattn_bk': (0.0, 2.0),
     'L1_xattn_bv': (0.0, 0.1),
     'L1_xattn_bo': (0.0, 0.1)}
    factors = {'L0_attn_w_attn': 3.624,
     'L0_attn_w_proj': 3.697,
     'L0_xattn_Wq': 8.0,
     'L0_xattn_Wk': 8.0,
     'L0_xattn_W_film_in': 3.433,
     'L0_xattn_W_film_out': 4.894,
     'L1_ffn_Wg': 3.862,
     'L1_ffn_W1': 8.0,
     'L1_ffn_b1': 8.0,
     'L1_ffn_W11': 8.0,
     'L1_ffn_b11': 8.0,
     'L1_ffn_W2': 8.0,
     'L1_ffn_b2': 16.993,
     'L1_ffn_Ws1': 4.868,
     'L1_ffn_bs1': 8.0,
     'L1_ffn_Ws11': 4.686,
     'L1_ffn_bs11': 8.0,
     'L1_ffn_Ws2': 4.808,
     'L1_ffn_bs2': 12.016}
    for name, (base, spread) in spreads.items():
        noise = np.random.default_rng([zlib.crc32(name.encode()), seed]).standard_normal(out[name].shape)
        drawn = base * np.exp(spread * noise) if base else spread * noise
        out[name] = jnp.asarray(drawn.astype(out[name].dtype))
    for name, factor in factors.items():
        out[name] = (out[name] * factor).astype(out[name].dtype)
    return out
```

```python
from contextlib import ExitStack

import numpy as np

import concourse.bass as bass
from concourse import mybir

F32 = mybir.dt.float32
BF16 = mybir.dt.bfloat16
U8 = mybir.dt.uint8
U32 = mybir.dt.uint32
ALU = mybir.AluOpType
ACT = mybir.ActivationFunctionType
AX = mybir.AxisListType

P = 128
B, T, C = 2, 512, 128
NT = B * T // P
HT = NT // B
BANKS = 8
F32R = mybir.dt.float32r
VERY_LOW = -3.0e38


def spread(ap, axis, shape):
    return ap.unsqueeze(axis).broadcast_to(shape)


def low_part(eng, low, x, high):
    return eng.tensor_tensor(low, x, high.bitcast(F32), ALU.subtract)


def three_passes(pe, out, weights, data, start, stop, **kw):
    for n, (w, d) in enumerate(((0, 0), (0, 1), (1, 0))):
        ins = pe.matmul(out, weights[w], data[d], start=(start and n == 0),
                        stop=(stop and n == 2), **kw)
    return ins


def load_exp_and_log(act):
    act.preload_act_table_set("natural_log_exp_and_others")


class Steps:

    def __init__(self, eng, sem, start):
        self.eng, self.sem, self.n = eng, sem, start

    def mark(self, ins):
        ins.then_inc(self.sem, 1)
        self.n += 1

    def wait(self):
        self.eng.wait_ge(self.sem, self.n)

    def __call__(self, ins):
        self.mark(ins)
        self.wait()


class Slot:
    def __init__(self, ps, filled, drained, use):
        self.ps, self.filled, self.drained, self.use = ps, filled, drained, use

    def claim(self, pe):
        if self.use > 1:
            pe.wait_ge(self.drained, self.use - 1)

    def ready(self, eng):
        eng.wait_ge(self.filled, self.use)

    def taken(self, eng):
        eng.wait_ge(self.drained, self.use)


class Ring:

    def __init__(self, core):
        self.core, self.uses = core, [0] * BANKS

    def plan(self, names, banks):
        out, at = {}, 0
        for name in names:
            k = banks[at % len(banks)]
            at += 1
            self.uses[k] += 1
            out[name] = Slot(self.core.bank[k], self.core.filled[k], self.core.drained[k], self.uses[k])
        return out


class Core:

    def __init__(self, nc, ctx, io):
        self.nc, self.ctx, self.io = nc, ctx, io
        self.bank = [ctx.enter_context(nc.psum_tensor(f"bank{k}", [P, 512], F32)) for k in range(BANKS)]
        self.filled = [self.sem(f"bank{k}_filled") for k in range(BANKS)]
        self.drained = [self.sem(f"bank{k}_drained") for k in range(BANKS)]
        self.ring = Ring(self)
        self.dve_step = self.sem("vector_step")
        self.act_step = self.sem("scalar_step")
        self.pool_step = self.sem("pool_step")
        self.count = {"dve": 0, "act": 0, "pool": 0}
        self.loaded = {}
        self.tiles = {}
        self.to_load = []

    def sem(self, name):
        return self.ctx.enter_context(self.nc.semaphore(name))

    def steps(self, eng, which):
        return Steps(eng, {"dve": self.dve_step, "act": self.act_step, "pool": self.pool_step}[which],
                     self.count[which])

    def keep(self, which, steps):
        self.count[which] = steps.n

    def tile(self, name, shape, dt=F32, ctx=None):
        return (ctx or self.ctx).enter_context(self.nc.sbuf_tensor(name, shape, dt))

    def resident(self, name, shape, dt=F32, ctx=None):
        self.tiles[name] = self.tile(name, shape, dt, ctx)
        return self.tiles[name]

    def issue_loads(self, sp):
        for group, dst, src in self.to_load:
            sp.dma_start(dst, src).then_inc(self.loaded[group][0], 16)
        self.to_load = []

    def wait_loaded(self, eng, *groups):
        for g in groups:
            sem, n = self.loaded[g]
            eng.wait_ge(sem, n)



class Norm:

    def __init__(self, core):
        self.core = core
        self.variance_ready = core.sem("variance_ready")
        self.root_ready = core.sem("root_ready")
        self.stats = core.tile("norm_stats", [P, 2, HT, 6])
        self.mean_var = core.tile("norm_mean_var", [P, 2, HT, 2])
        self.var = core.tile("norm_var", [P, 2, HT])
        self.log = core.tile("norm_log", [P, 2, HT])
        self.root = core.tile("norm_root", [P, 2, HT])
        self.square = core.tile("norm_square", [P, 2, HT])
        self.on_dve = self.on_act = 0

    def dve(self, dve, step, src, dst, eps=1e-5):
        k = self.on_dve % 2
        self.on_dve += 1
        var, root, square = self.var[:, k], self.root[:, k], self.square[:, k]
        for i in range(HT):
            step.mark(dve.bn_stats(self.stats[:, k, i], src[:, i]))
        step.wait()
        for i in range(HT):
            step.mark(dve.bn_aggr(self.mean_var[:, k, i], self.stats[:, k, i]))
        step.wait()
        dve.tensor_scalar(var, self.mean_var[:, k, :, 1], eps, None, ALU.add).then_inc(self.variance_ready, 1)
        dve.wait_ge(self.root_ready, self.on_dve)
        step(dve.tensor_tensor(square, root, root, ALU.mult))
        step(dve.scalar_tensor_tensor(square, square, -0.5, var, ALU.mult, ALU.mult))
        step(dve.scalar_tensor_tensor(root, square, 1.5, root, ALU.add, ALU.mult))
        for i in range(HT):
            step.mark(dve.tensor_scalar(dst[:, i], src[:, i], self.mean_var[:, k, i, 0:1], root[:, i:i + 1],
                                        ALU.subtract, ALU.mult))

    def act(self, act, step):
        k = self.on_act % 2
        self.on_act += 1
        act.wait_ge(self.variance_ready, self.on_act)
        step(act.activation(self.log[:, k], self.var[:, k], ACT.Ln))
        act.activation(self.root[:, k], self.log[:, k], ACT.Exp, scale=-0.5).then_inc(self.root_ready, 1)




KEPT = ("ident", "rows", "cols", "head_of", "ctxT")


def load_all(core, x):
    io = core.io
    plan = [("lin", "ident", None, F32, None)]
    plan += [("x", x[:, HT * b:HT * b + HT], io["x"][b].rearrange("(i p) c -> p i c", p=P)) for b in range(B)]
    plan += [("lin", n, None, F32, None) for n in ("w_attn", "head_of", "causal", "head_block", "lin_w_proj")]
    plan += [("ssk", "modes", None, F32, None),
             ("ssk", "log_dt", [P, P], F32, io["log_dt"].partition_broadcast(P))]
    plan += [("ssk", n, None, F32, None) for n in ("ssk_phase", "lag_a", "lag_b")]
    plan += [("xa", "rows", [P, io["rows"].shape[0]], F32, io["rows"].partition_broadcast(P)),
             ("xa", "cols", None, F32, None)]
    plan += [("xa", n, None, F32, None)
             for n in ("xa_wq", "xa_wk", "xa_wv", "ctxT", "head4_of", "xa_wfilm", "film_bias", "xa_w1")]
    plan += [("xa", "xa_w2", [P, 4, P], F32, io["xa_w2"].rearrange("(j p) c -> p j c", p=P)),
             ("xa", "mask_ctx", [P, B, G], U8, io["mask_ctx"].partition_broadcast(P)),
             ("xa", "mask_text", None, U8, None)]
    plan += [("ea", "sim", None, F32, None), ("ea", "expert_row", None, BF16, io["expert_row"].bitcast(BF16)),
             ("ea", "expert_pair", None, BF16, io["expert_pair"].bitcast(BF16)), ("ea", "causal_bias", None, F32, None),
             ("ea", "w_qkv", None, F32, None),
             ("ea", "w_o", [P, NE // 2, P], F32, io["w_o"].rearrange("(j e) d c -> (e d) j c", e=2))]
    for place in (core.ctx, core.experts, core.early):
        for group, name, *rest in plan:
            own = core.ctx if name in KEPT else core.experts if group == "ea" else core.early
            if group != "x" and own is place:
                shape, dt, _ = rest
                core.resident(name, shape or list(io[name].shape), dt, place)
    for name in ("taps", "kernel_re", "kernel_im"):
        core.resident(name, [P, LT, P], F32, core.early)
    core.resident("far", [P, P, LA], F32, core.early)
    core.resident("near", [P, P, LB], F32, core.early)
    send(core, [p if p[0] == "x" else (p[0], whole(core.tiles[p[1]]), io[p[1]] if p[4] is None else p[4])
                for p in plan])


def load_waves(core):
    plan = []
    for group, names in (("kernel_dft", ("cos_lag", "sin_lag")), ("dft", ("cos_half", "sin_half"))):
        for name in names:
            core.resident(name, [P, LT, T], F32, core.early)
            plan.append((group, core.tiles[name][:, :, :], core.io[name].rearrange("(l p) f -> p l f", p=P)))
    send(core, plan)


def whole(tile):
    return tile[tuple(slice(None) for _ in tile.shape)]


def late(core, plan, group, name, shape=None, dt=F32, src=None):
    src = core.io[name] if src is None else src
    core.resident(name, list(shape or src.shape), dt, core.late)
    plan.append((group, whole(core.tiles[name]), src))


def load_gated(core):
    io, plan = core.io, []
    for name in ("ga_vcT", "ga_wqv", "ga_wkk", "ga_wa", "restart"):
        late(core, plan, "ga", name)
    late(core, plan, "ga", "ga_qc", [HC, NP, 2 * HC])
    late(core, plan, "ga", "ga_wo", [HV, NH, P], src=io["ga_wo"].rearrange("(h v) c -> v h c", v=HV))
    late(core, plan, "ga", "causal_bits", [P, NP, P], U32)
    send(core, plan)


def load_last(core):
    io, plan = core.io, []
    for name in ("ca_wk", "ca_wv", "ca_wq", "ca_wo"):
        late(core, plan, "ca", name)
    for name in ("em_wg", "em_b2"):
        late(core, plan, "em", name)
    for n, units in enumerate(EM_LOADS):
        if n == 0:
            for name, shape, dt in (("em_up", [P, NU, 2 * HE], F32), ("em_up_high", [P, NU, 2 * HE], F32R),
                                    ("em_up_low", [P, NU, 2 * HE], F32R), ("em_down", [P, NU, 2, P], F32)):
                core.resident(name, shape, dt, core.late)
        for name in ("em_up", "em_down"):
            plan.append((f"em_{n}", core.tiles[name][:, units], io[name][:, units]))
    send(core, plan)


def send(core, plan):
    counts = {}
    for group, _, _ in plan:
        counts[group] = counts.get(group, 0) + 16
    for group, n in counts.items():
        core.loaded[group] = (core.sem(f"{group}_loaded"), n)
    core.to_load += plan



def linear_attention(core, x, out):
    nc = core.nc
    H, D = 16, C // 16
    E = D + 1
    with ExitStack() as ctx:
        def sb(name, shape, dt=F32):
            return core.tile("lin_" + name, shape, dt, ctx)

        def sem(name):
            return ctx.enter_context(nc.semaphore("lin_" + name))

        w_attn, w_proj = core.tiles["w_attn"], core.tiles["lin_w_proj"]
        ident, causal = core.tiles["ident"], core.tiles["causal"]
        head_of, head_block = core.tiles["head_of"], core.tiles["head_block"]
        xT = sb("xT", [P, NT, P])
        qT = sb("qT", [P, NT, P])
        kT = sb("kT", [P, NT, P])
        k_rows = sb("k_rows", [P, NT, P])
        v_one = sb("v_one", [P, NT, H, E])
        exp_of = sb("exp_of", [P, 2, 512])
        relu_of = sb("relu_of", [P, 2, 512])
        q_wide = sb("q_wide", [P, 2, H, P])
        scores = sb("scores", [P, 2, H, P])
        state = sb("state", [P, 2, H, E])
        den = sb("den", [P, 2, H])
        y = sb("y", [P, 2, P])
        yT = sb("yT", [P, 2, P])
        res = sb("res", [P, NT, P])

        features = []
        for b in range(B):
            lo, hi = HT * b, HT * b + HT
            features += [(f"q{b}", qT[:, lo:hi], P), (f"k{b}", kT[:, lo:hi], P),
                         (f"ks{b}0", k_rows[:, lo:lo + 2], None), (f"ks{b}1", k_rows[:, lo + 2:hi], None)]
        plan = []
        for b in range(B):
            plan += [f"xT{b}", f"q{b}", f"k{b}", f"ks{b}0", f"ks{b}1"]
        plan += [f"sc0_{c}" for c in range(4)]
        for g in range(NT):
            if g + 1 < NT:
                plan += [f"sc{g + 1}_{c}" for c in range(4)]
            plan += [f"y{g}"] + ([f"yT{g - 1}", f"o{g - 1}"] if g else [])
        plan += [f"yT{NT - 1}", f"o{NT - 1}"]
        ring = core.ring.plan(plan, range(BANKS - 1))
        running = core.bank[BANKS - 1][:, 0:H * E]

        ones_ready = sem("ones_ready")
        elu_exp = sem("elu_exp")
        k_rows_relu = sem("k_rows_relu")
        elu_done = sem("elu_done")
        v_ready = sem("v_ready")
        wide_ready = sem("wide_ready")
        summed = sem("summed")
        state_ready = sem("state_ready")

        kernel = core.kernel = StateSpaceKernel(core, ctx)

        with nc.Block() as block:
            @block.sync
            def _(sp):
                core.issue_loads(sp)

            @block.tensor
            def _(pe):
                core.wait_loaded(pe, "x", "lin")
                for b in range(B):
                    s = ring[f"xT{b}"]
                    s.claim(pe)
                    for i in range(HT):
                        ins = pe.transpose(s.ps[:, i * P:(i + 1) * P], x[:, HT * b + i], ident[:, :])
                    ins.then_inc(s.filled, 1)
                    s.taken(pe)
                    for n, name in enumerate([f"q{b}", f"k{b}"]):
                        s = ring[name]
                        s.claim(pe)
                        pe.matmul(s.ps[:, :], w_attn[:, n * P:(n + 1) * P], xT[:, HT * b:HT * b + HT],
                                  start=True, stop=True).then_inc(s.filled, 1)
                    for half in range(2):
                        s = ring[f"ks{b}{half}"]
                        s.claim(pe)
                        for i in range(2):
                            ins = pe.matmul(s.ps[:, 2 * i * P:2 * (i + 1) * P], xT[:, HT * b + 2 * half + i],
                                            w_attn[:, P:3 * P], start=True, stop=True)
                        ins.then_inc(s.filled, 1)

                def weigh(g):
                    pe.wait_ge(elu_done, 4 * (g // HT) + 4)
                    pe.wait_ge(wide_ready, g + 1)
                    for c in range(4):
                        s = ring[f"sc{g}_{c}"]
                        s.claim(pe)
                        pe.matmul(s.ps[:, :], kT[:, g], q_wide[:, g % 2, 4 * c:4 * c + 4], start=True,
                                  stop=True).then_inc(s.filled, 1)

                def gather(g):
                    s = ring[f"y{g}"]
                    s.claim(pe)
                    pe.wait_ge(v_ready, 2 * (g // HT) + 2)
                    if g % HT:
                        pe.wait_ge(state_ready, g - g // HT)
                        pe.matmul(s.ps[:, 0:H * E], qT[:, g], state[:, g % 2], start=True, stop=False,
                                  skip_group_check=True)
                    for h in range(H):
                        if h % 4 == 0:
                            ring[f"sc{g}_{h // 4}"].taken(pe)
                        ins = pe.matmul(s.ps[:, h * E:(h + 1) * E], scores[:, g % 2, h], v_one[:, g, h],
                                        start=(h == 0 and g % HT == 0), stop=(h == H - 1), skip_group_check=True)
                    ins.then_inc(s.filled, 1)
                    if g % HT < HT - 1:
                        if g == HT:
                            pe.wait_ge(state_ready, HT - 1)
                        pe.matmul(running, k_rows[:, g], v_one[:, g], start=(g % HT == 0), stop=True,
                                  skip_group_check=True).then_inc(summed, 1)

                def project(g):
                    s, o = ring[f"yT{g}"], ring[f"o{g}"]
                    ring[f"y{g}"].taken(pe)
                    s.claim(pe)
                    pe.transpose(s.ps[:, 0:P], y[:, g % 2], ident[:, :]).then_inc(s.filled, 1)
                    o.claim(pe)
                    s.taken(pe)
                    pe.matmul(o.ps[:, 0:P], yT[:, g % 2], w_proj[:, :], start=True, stop=True).then_inc(o.filled, 1)

                weigh(0)
                for g in range(NT):
                    if g + 1 < NT:
                        weigh(g + 1)
                    gather(g)
                    if g:
                        project(g - 1)
                project(NT - 1)

            @block.scalar
            def _(act):
                step = core.steps(act, "act")
                load_exp_and_log(act)
                for b in range(B):
                    s = ring[f"xT{b}"]
                    s.ready(act)
                    act.copy(xT[:, HT * b:HT * b + HT], s.ps[:, :]).then_inc(s.drained, 1)
                    for n in range(4 * b, 4 * b + 4):
                        name, _, _ = features[n]
                        s = ring[name]
                        s.ready(act)
                        if n >= 2:
                            act.wait_ge(elu_done, n - 1)
                        src = s.ps[:, :]
                        if name[1] == "s":
                            src = s.ps[:, :].rearrange("p (i n) -> p i n", i=2)[:, :, 0:P]
                        w = 512 if name[1] != "s" else 2 * P
                        act.activation(exp_of[:, n % 2, 0:w], src, ACT.Exp).then_inc(elu_exp, 1)
                        ins = act.activation(relu_of[:, n % 2, 0:w], src, ACT.Relu)
                        if name[1] != "s":
                            ins.then_inc(s.drained, 1)
                        else:
                            ins.then_inc(k_rows_relu, 1)
                            act.wait_ge(ones_ready, 1)
                            g = HT * b + 2 * (int(name[3]))
                            for i in range(2):
                                act.copy(v_one[:, g + i, :, 0:D],
                                         s.ps[:, (2 * i + 1) * P:(2 * i + 2) * P].rearrange("p (h d) -> p h d", h=H)
                                         ).then_inc(v_ready if i == 0 else s.drained, 1)
                kernel.exps_and_sines(act)
                for g in range(NT):
                    if g in (2, 3):
                        kernel.far_sine(act, g - 2)
                    if g == HT - 1:
                        load_exp_and_log(act)
                    s = ring[f"yT{g}"]
                    s.ready(act)
                    act.copy(yT[:, g % 2], s.ps[:, 0:P]).then_inc(s.drained, 1)
                    if g % HT == HT - 1:
                        core.norm.act(act, step)
                core.keep("act", step)

            @block.gpsimd
            def _(pool):
                pool.memset(v_one[:, :, :, D:E], 1.0).then_inc(ones_ready, 1)
                core.wait_loaded(pool, "lin")
                for g in range(NT):
                    if g in (2, 3):
                        kernel.far_angles(pool, g - 2)
                    pool.wait_ge(elu_done, 4 * (g // HT) + 1)
                    if g >= 2:
                        pool.wait_ge(ring[f"sc{g - 2}_3"].filled, ring[f"sc{g - 2}_3"].use)
                    pool.tensor_tensor(q_wide[:, g % 2], spread(qT[:, g], 1, [P, H, P]),
                                       spread(head_of[:, :], 2, [P, H, P]), ALU.mult).then_inc(wide_ready, 1)

            @block.vector
            def _(dve):
                step = core.steps(dve, "dve")
                core.wait_loaded(dve, "x", "lin")
                rows = 0
                for n, (name, dst, _) in enumerate(features):
                    dve.wait_ge(elu_exp, n + 1)
                    if name[1] != "s":
                        ring[name].taken(dve)
                        w = 512
                    else:
                        rows += 1
                        dve.wait_ge(k_rows_relu, rows)
                        w = 2 * P
                    dve.scalar_tensor_tensor(dst, exp_of[:, n % 2, 0:w].rearrange("p (a c) -> p a c", c=P), 1.0,
                                             relu_of[:, n % 2, 0:w].rearrange("p (a c) -> p a c", c=P),
                                             ALU.min, ALU.add).then_inc(elu_done, 1)

                def mask(g):
                    for c in range(4):
                        s = ring[f"sc{g}_{c}"]
                        s.ready(dve)
                        if g >= 2 and c == 0:
                            dve.wait_ge(ring[f"y{g - 2}"].filled, ring[f"y{g - 2}"].use)
                        dve.tensor_tensor(scores[:, g % 2, 4 * c:4 * c + 4],
                                          s.ps[:, :].rearrange("p (h t) -> p h t", h=4),
                                          spread(causal[:, :], 1, [P, 4, P]), ALU.mult).then_inc(s.drained, 1)

                def carry(g):
                    if g % HT == HT - 1:
                        return
                    dve.wait_ge(summed, g - g // HT + 1)
                    dve.tensor_tensor(state[:, (g + 1) % 2].rearrange("p h e -> p (h e)"), running,
                                      head_block[:, :], ALU.mult).then_inc(state_ready, 1)

                def divide(g):
                    s = ring[f"y{g}"]
                    s.ready(dve)
                    num = s.ps[:, 0:H * E].rearrange("p (h e) -> p h e", e=E)
                    step(dve.tensor_scalar(den[:, g % 2], num[:, :, D], 1e-6, None, ALU.add))
                    step(dve.reciprocal(den[:, g % 2], den[:, g % 2]))
                    if g >= 2:
                        dve.wait_ge(ring[f"yT{g - 2}"].filled, ring[f"yT{g - 2}"].use)
                    dve.tensor_tensor(y[:, g % 2].rearrange("p (h d) -> p h d", h=H), num[:, :, 0:D],
                                      spread(den[:, g % 2], 2, [P, H, D]), ALU.mult).then_inc(s.drained, 1)

                def add(g):
                    s = ring[f"o{g}"]
                    s.ready(dve)
                    dve.tensor_tensor(res[:, g], s.ps[:, 0:P], x[:, g], ALU.add).then_inc(s.drained, 1)
                    if g % HT == HT - 1:
                        s.taken(dve)
                        lo = g - HT + 1
                        core.norm.dve(dve, step, res[:, lo:g + 1], out[:, lo:g + 1])

                kernel_steps = [(kernel.near_angles,), (), (kernel.far_fraction,), (kernel.far_fraction,),
                                (kernel.weights,), (kernel.near_product,), (kernel.far_product,),
                                (kernel.far_product,)]
                kernel.turns(dve, step)
                mask(0)
                for g in range(NT):
                    if g + 1 < NT:
                        mask(g + 1)
                    for part in kernel_steps[g]:
                        part(dve, step)
                    carry(g)
                    divide(g)
                    if g:
                        add(g - 1)
                add(NT - 1)
                step.wait()
                core.keep("dve", step)



NMODE, HD2, G = 64, 32, 77
LA, LB = 32, 16
LT = T // P
ROUND = 12582912.0
SELECTED = -3.3e38
K_TOP = 32


class StateSpaceKernel:

    def __init__(self, core, ctx):
        def sb(name, shape, dt=F32):
            return core.tile("ssk_" + name, shape, dt, ctx)

        def sem(name):
            return ctx.enter_context(core.nc.semaphore("ssk_" + name))

        self.core, self.t = core, core.tiles
        self.dt = sb("dt", [P, P])
        self.zr = sb("zr", [P, P])
        self.turn = sb("turn", [P, P])
        self.small = [sb(f"small{n}", [P, P]) for n in range(10)]
        self.far = self.t["far"]
        self.near = self.t["near"]
        self.angle = [sb(f"far_angle{n}", [P, P // 2, LA]) for n in range(2)]
        self.wave = [sb(f"near_wave{n}", [P, P, LB]) for n in range(2)]
        self.whole = sb("whole", [P, P * LB])
        self.scratch = core.nc.dram_tensor("kernel_taps", [T, C], F32, kind="Internal").ap()
        self.dt_ready, self.tanh_ready = sem("dt_ready"), sem("tanh_ready")
        self.z_ready, self.turn_ready = sem("z_ready"), sem("turn_ready")
        self.angle_ready = sem("angle_ready")
        self.small_fraction, self.near_fraction, self.far_fraction_ready = (
            sem("small_fraction"), sem("near_fraction"), sem("far_fraction"))
        self.small_sines, self.near_sines, self.far_sines = sem("small_sines"), sem("near_sines"), sem("far_sines")
        self.near_sizes, self.far_sizes = sem("near_sizes"), sem("far_sizes")
        self.near_done, self.far_done = core.sem("near_done"), core.sem("far_done")
        self.taps_out, self.taps_in = core.sem("taps_out"), core.sem("taps_in")
        self.fractions = self.products = 0

    def half(self, n):
        return slice(n * P // 2, (n + 1) * P // 2)


    def far_angles(self, pool, n):
        shape = [P, P // 2, LA]
        if n == 0:
            self.core.wait_loaded(pool, "ssk")
            pool.wait_ge(self.turn_ready, 1)
        pool.tensor_tensor(self.angle[n][:, :, :], spread(self.turn[:, self.half(n)], 2, shape),
                           spread(self.t["lag_a"][:, :], 1, shape), ALU.mult).then_inc(self.angle_ready, 1)


    def exps_and_sines(self, act):
        self.core.wait_loaded(act, "ssk")
        zr, small = self.zr, self.small
        act.activation(self.dt[:, :], self.t["log_dt"][:, :], ACT.Exp).then_inc(self.dt_ready, 1)
        act.wait_ge(self.z_ready, 1)
        for b in range(LB):
            act.activation(self.near[:, :, b], zr[:, :], ACT.Exp, scale=float(b)).then_inc(self.near_sizes, 1)
        for a in range(LA):
            act.activation(self.far[:, :, a], zr[:, :], ACT.Exp, scale=float(LB * a)).then_inc(self.far_sizes, 1)
        act.preload_act_table_set("silu_and_others")
        act.activation(small[0][:, :], zr[:, :], ACT.Tanh, scale=0.5).then_inc(self.tanh_ready, 1)
        turn = float(2 * np.pi)
        act.wait_ge(self.small_fraction, 1)
        act.activation(small[2][:, :], small[1][:, :], ACT.Sin, scale=turn).then_inc(self.small_sines, 1)
        act.activation(small[3][:, :], small[1][:, :], ACT.Sin, scale=turn / 2).then_inc(self.small_sines, 1)
        for n, wave in enumerate(self.wave):
            act.wait_ge(self.near_fraction, n + 1)
            act.activation(wave[:, :, :], wave[:, :, :], ACT.Sin, scale=turn).then_inc(self.near_sines, 1)

    def far_sine(self, act, n):
        angle = self.angle[n][:, :, :]
        act.wait_ge(self.far_fraction_ready, n + 1)
        act.activation(angle, angle, ACT.Sin, scale=float(2 * np.pi)).then_inc(self.far_sines, 1)


    def fraction(self, dve, step, x, whole, offset=None):
        if offset is not None:
            step(dve.tensor_scalar(x, x, offset, None, ALU.add))
        step(dve.tensor_scalar(whole, x, ROUND, ROUND, ALU.add, ALU.subtract))
        return dve.tensor_tensor(x, x, whole, ALU.subtract)

    def turns(self, dve, step):
        are, aim = self.t["modes"][:, 0], self.t["modes"][:, 1]
        turn, small = self.turn[:, :], self.small
        self.core.wait_loaded(dve, "ssk")
        dve.wait_ge(self.dt_ready, 1)
        dve.tensor_tensor(self.zr[:, :], self.dt[:, :], are, ALU.mult).then_inc(self.z_ready, 1)
        step(dve.tensor_tensor(turn, self.dt[:, :], aim, ALU.mult))
        dve.tensor_scalar(turn, turn, float(1 / (2 * np.pi)), None, ALU.mult).then_inc(self.turn_ready, 1)
        dve.wait_ge(self.turn_ready, 1)
        step(dve.tensor_copy(small[1][:, :], turn))
        self.fraction(dve, step, small[1][:, :], small[4][:, :]).then_inc(self.small_fraction, 1)

    def near_angles(self, dve, step):
        shape, phase = [P, P, LB], self.t["ssk_phase"]
        w = [x[:, :, :].rearrange("p d b -> p (d b)") for x in self.wave]
        step(dve.tensor_tensor(self.wave[0][:, :, :], spread(self.turn[:, :], 2, shape),
                               spread(self.t["lag_b"][:, :], 1, shape), ALU.mult))
        step(dve.tensor_scalar(w[1], w[0], phase[:, 2:3], None, ALU.add))
        self.fraction(dve, step, w[0], self.whole[:, :], phase[:, 1:2]).then_inc(self.near_fraction, 1)
        dve.wait_ge(self.near_fraction, 1)
        self.fraction(dve, step, w[1], self.whole[:, :]).then_inc(self.near_fraction, 1)
        dve.wait_ge(self.near_fraction, 2)

    def far_fraction(self, dve, step):
        n = self.fractions
        self.fractions += 1
        dve.wait_ge(self.angle_ready, n + 1)
        self.fraction(dve, step, self.angle[n][:, :, :].rearrange("p d a -> p (d a)"), self.whole[:, :],
                      self.t["ssk_phase"][:, 0:1]).then_inc(self.far_fraction_ready, 1)
        dve.wait_ge(self.far_fraction_ready, n + 1)

    def weights(self, dve, step):
        dve.wait_ge(self.tanh_ready, 1)
        dve.wait_ge(self.small_sines, 2)
        are, aim, cre, cim = (self.t["modes"][:, n] for n in range(4))
        th, sin, half, em, cm, re, im, nr, ni, q = (self.small[n][:, :] for n in (0, 2, 3, 4, 5, 6, 7, 8, 9, 1))
        step(dve.tensor_scalar(em, th, -1.0, 1.0, ALU.mult, ALU.add))
        step(dve.reciprocal(em, em))
        step(dve.scalar_tensor_tensor(em, th, 2.0, em, ALU.mult, ALU.mult))
        step(dve.scalar_tensor_tensor(cm, half, -2.0, half, ALU.mult, ALU.mult))
        step(dve.scalar_tensor_tensor(re, cm, 1.0, em, ALU.add, ALU.mult))
        step(dve.tensor_tensor(re, re, cm, ALU.add))
        step(dve.scalar_tensor_tensor(im, em, 1.0, sin, ALU.add, ALU.mult))
        step(dve.tensor_tensor(nr, cre, re, ALU.mult))
        step(dve.tensor_tensor(q, cim, im, ALU.mult))
        step(dve.tensor_tensor(nr, nr, q, ALU.subtract))
        step(dve.tensor_tensor(ni, cre, im, ALU.mult))
        step(dve.tensor_tensor(q, cim, re, ALU.mult))
        step(dve.tensor_tensor(ni, ni, q, ALU.add))
        step(dve.tensor_tensor(re, are, are, ALU.mult))
        step(dve.tensor_tensor(im, aim, aim, ALU.mult))
        step(dve.tensor_tensor(re, re, im, ALU.add))
        step(dve.reciprocal(re, re))
        step(dve.tensor_tensor(cm, nr, are, ALU.mult))
        step(dve.tensor_tensor(q, ni, aim, ALU.mult))
        step(dve.tensor_tensor(cm, cm, q, ALU.add))
        step(dve.scalar_tensor_tensor(cm, cm, 2.0, re, ALU.mult, ALU.mult))
        step(dve.tensor_tensor(em, ni, are, ALU.mult))
        step(dve.tensor_tensor(q, nr, aim, ALU.mult))
        step(dve.tensor_tensor(em, em, q, ALU.subtract))
        step(dve.scalar_tensor_tensor(em, em, 2.0, re, ALU.mult, ALU.mult))

    def near_product(self, dve, step):
        shape = [P, P, LB]
        re, im = self.small[5][:, :], self.small[4][:, :]
        w = [x[:, :, :] for x in self.wave]
        dve.wait_ge(self.near_sines, 2)
        step.mark(dve.tensor_tensor(w[0], w[0], spread(re, 2, shape), ALU.mult))
        step(dve.tensor_tensor(w[1], w[1], spread(im, 2, shape), ALU.mult))
        step(dve.tensor_tensor(w[0], w[0], w[1], ALU.add))
        dve.wait_ge(self.near_sizes, LB)
        dve.tensor_tensor(self.near[:, :, :], w[0], self.near[:, :, :], ALU.mult).then_inc(self.near_done, 1)

    def far_product(self, dve, step):
        n = self.products
        self.products += 1
        dve.wait_ge(self.far_sines, n + 1)
        dve.wait_ge(self.far_sizes, LA)
        far = self.far[:, self.half(n)]
        dve.tensor_tensor(far, self.angle[n][:, :, :], far, ALU.mult).then_inc(self.far_done, 1)


    def multiply(self, pe, slot):
        slot.claim(pe)
        pe.wait_ge(self.near_done, 1)
        pe.wait_ge(self.far_done, 2)
        for d in range(P // 4):
            for j in range(4):
                ins = pe.matmul(slot.ps[32 * j:32 * j + LA, d * LB:(d + 1) * LB], self.far[:, 32 * j + d],
                                self.near[:, 32 * j + d], start=True, stop=True, skip_group_check=True)
        ins.then_inc(slot.filled, 1)


    def turn_lags(self, sp, slot, lags):
        slot.taken(sp)
        for j in range(4):
            sp.dma_start(self.scratch[:, 32 * j:32 * j + 32].rearrange("(a b) d -> a b d", b=LB),
                         lags[32 * j:32 * j + 32]).then_inc(self.taps_out, 16)
        sp.wait_ge(self.taps_out, 64)
        sp.dma_start(self.t["taps"][:, :, :], self.scratch.rearrange("(l p) d -> p l d", p=P)
                     ).then_inc(self.taps_in, 16)
        sp.wait_ge(self.taps_in, 16)


def cross_attention_ssm(core, x, out):
    nc = core.nc
    t = core.tiles
    H = 4
    with ExitStack() as ctx:
        def sb(name, shape, dt=F32):
            return core.tile("xa_" + name, shape, dt, ctx)

        def sem(name):
            return ctx.enter_context(nc.semaphore("xa_" + name))

        ident = t["ident"]
        rows = {n: t["rows"][:, a:b] for n, (a, b) in core.rows.items()}
        bias = {n: t["cols"][:, a:b] for n, (a, b) in core.cols.items()}
        xT = sb("xT", [P, NT, P])
        qT = sb("qT", [P, NT, P])
        x_bias = qT
        k_wide = sb("k_wide", [P, B, H, G])
        v = sb("v", [G, B, P])
        mask_bias = sb("mask_bias", [P, B, G])
        text_weight = sb("text_weight", [P, NT])
        ones = sb("ones", [1, P])
        score = sb("score", [P, 2, H, G])
        left = sb("left", [P, 2, H, G])
        top = sb("top", [P, 2, 4, H, 8])
        prob = sb("prob", [P, 2, H, G])
        total = sb("total", [P, 2, H])
        mean = sb("mean", [P, NT, G])
        meanT = sb("meanT", [G, NT, P])
        cT = sb("cT", [P, NT, P])
        film = sb("film", [P, NT, 4, P])
        u = sb("u", [P, NT, P])
        yr, yi = sb("yr", [P, LT, P]), sb("yi", [P, LT, P])
        part = [sb(f"part{n}", [P, LT, P]) for n in range(4)]
        xt = sb("xt", [P, NT, P])
        lags = sb("lags", [P, LB, HD2])
        h = sb("h", [P, NT, P])
        hT = xT
        up = sb("up", [P, 4, NT, P])

        plan = ["keys", "values"]
        for b in range(B):
            plan += [f"xT{b}", f"q{b}"]
        plan += [f"s{g}" for g in range(NT)] + ["taps", "kernel_re", "kernel_im"]
        work = {b: {"film": [f"meanT{b}", f"c{b}"] + [f"film{g}" for g in range(HT * b, HT * b + HT)],
                    "forth": [f"xr{b}", f"xi{b}"], "back": [f"y{b}"],
                    "up": [f"hT{b}"] + [f"up{b}{j}" for j in range(4)], "down": [f"down{b}"]} for b in range(B)}
        order = [("film", 0), ("forth", 0), ("back", 0), ("film", 1), ("forth", 1), ("up", 0), ("back", 1),
                 ("down", 0), ("up", 1), ("down", 1)]
        for stage, b in order:
            plan += work[b][stage]
        ring = core.ring.plan(plan, range(BANKS))

        consts_ready = sem("consts_ready")
        shifted = sem("shifted")
        exps = sem("exps")
        mean_ready = sem("mean_ready")
        weighed, total_ready = sem("weighed"), sem("total_ready")
        film_ready = sem("film_ready")
        normed = sem("normed")
        u_ready = sem("u_ready")
        x_bias_ready = sem("x_bias_ready")
        skip_ready = sem("skip_ready")
        part_ready, y_ready = sem("part_ready"), sem("y_ready")
        biased = sem("biased")
        xt_ready = sem("xt_ready")
        h_ready = sem("h_ready")

        def half(b):
            return slice(HT * b, HT * b + HT)

        with nc.Block() as block:
            @block.sync
            def _(sp):
                core.issue_loads(sp)
                core.kernel.turn_lags(sp, ring["taps"], lags)

            @block.tensor
            def _(pe):
                core.wait_loaded(pe, "xa")
                s = ring["keys"]
                s.claim(pe)
                pe.matmul(s.ps[:, 0:B * G], t["xa_wk"][:, :], t["ctxT"][:, :, :], start=True,
                          stop=True).then_inc(s.filled, 1)
                s = ring["values"]
                s.claim(pe)
                for b in range(B):
                    ins = pe.matmul(s.ps[0:G, b * P:(b + 1) * P], t["ctxT"][:, b], t["xa_wv"][:, :], start=True,
                                    stop=True)
                ins.then_inc(s.filled, 1)
                for b in range(B):
                    s = ring[f"xT{b}"]
                    s.claim(pe)
                    for i in range(HT):
                        ins = pe.transpose(s.ps[:, i * P:(i + 1) * P], x[:, HT * b + i], ident[:, :])
                    ins.then_inc(s.filled, 1)
                    s.taken(pe)
                    s = ring[f"q{b}"]
                    s.claim(pe)
                    pe.matmul(s.ps[:, :], t["xa_wq"][:, :], xT[:, half(b)], start=True,
                              stop=True).then_inc(s.filled, 1)
                ring["keys"].taken(pe)
                pe.wait_ge(consts_ready, 2)
                for g in range(NT):
                    if g % HT == 0:
                        ring[f"q{g // HT}"].taken(pe)
                    s = ring[f"s{g}"]
                    s.claim(pe)
                    pe.matmul(s.ps[:, 0:H * G], qT[:, g], k_wide[:, g // HT], start=True,
                              stop=True).then_inc(s.filled, 1)
                core.kernel.multiply(pe, ring["taps"])
                core.wait_loaded(pe, "kernel_dft")
                pe.wait_ge(core.kernel.taps_in, 16)
                for name, w in (("kernel_re", t["cos_lag"]), ("kernel_im", t["sin_lag"])):
                    s = ring[name]
                    s.claim(pe)
                    for f in range(LT):
                        for l in range(LT):
                            ins = pe.matmul(s.ps[:, f * P:(f + 1) * P], w[:, l, f * P:(f + 1) * P], t["taps"][:, l],
                                            start=(l == 0), stop=(l == LT - 1), skip_group_check=True)
                    ins.then_inc(s.filled, 1)
                ring["values"].taken(pe)
                pe.wait_ge(consts_ready, 5)

                def film_of(b):
                    s = ring[f"meanT{b}"]
                    s.claim(pe)
                    for i in range(HT):
                        pe.wait_ge(mean_ready, HT * b + i + 1)
                        ins = pe.transpose(s.ps[0:G, i * P:(i + 1) * P], mean[:, HT * b + i], ident[:, :])
                    ins.then_inc(s.filled, 1)
                    s.taken(pe)
                    s = ring[f"c{b}"]
                    s.claim(pe)
                    pe.matmul(s.ps[:, :], v[:, b], meanT[:, half(b)], start=True, stop=True).then_inc(s.filled, 1)
                    s.taken(pe)
                    for g in range(HT * b, HT * b + HT):
                        s = ring[f"film{g}"]
                        s.claim(pe)
                        pe.matmul(s.ps[:, :], cT[:, g], t["xa_wfilm"][:, :], start=True, stop=False)
                        pe.matmul(s.ps[:, :], ones[:, :], t["film_bias"][:, :], start=False,
                                  stop=True).then_inc(s.filled, 1)

                def forth(b):
                    core.wait_loaded(pe, "dft")
                    pe.wait_ge(u_ready, b + 1)
                    for name, w in ((f"xr{b}", t["cos_half"]), (f"xi{b}", t["sin_half"])):
                        s = ring[name]
                        s.claim(pe)
                        for f in range(LT):
                            for i in range(LT):
                                ins = pe.matmul(s.ps[:, f * P:(f + 1) * P], w[:, i, f * P:(f + 1) * P],
                                                u[:, HT * b + i], start=(i == 0), stop=(i == LT - 1),
                                                skip_group_check=True)
                        ins.then_inc(s.filled, 1)

                def back(b):
                    pe.wait_ge(y_ready, 2 * b + 2)
                    s = ring[f"y{b}"]
                    s.claim(pe)
                    for l in range(LT):
                        for f in range(LT):
                            for w, src, first in ((t["cos_half"], yr, True), (t["sin_half"], yi, False)):
                                ins = pe.matmul(s.ps[:, l * P:(l + 1) * P], w[:, f, l * P:(l + 1) * P], src[:, f],
                                                start=(f == 0 and first), stop=(f == LT - 1 and not first),
                                                skip_group_check=True)
                    ins.then_inc(s.filled, 1)

                def up_of(b):
                    pe.wait_ge(h_ready, b + 1)
                    s = ring[f"hT{b}"]
                    s.claim(pe)
                    for i in range(HT):
                        ins = pe.transpose(s.ps[:, i * P:(i + 1) * P], h[:, HT * b + i], ident[:, :])
                    ins.then_inc(s.filled, 1)
                    s.taken(pe)
                    for j in range(4):
                        s = ring[f"up{b}{j}"]
                        s.claim(pe)
                        pe.matmul(s.ps[:, :], t["xa_w1"][:, j * P:(j + 1) * P], hT[:, half(b)], start=True,
                                  stop=True).then_inc(s.filled, 1)

                def down(b):
                    s = ring[f"down{b}"]
                    s.claim(pe)
                    for j in range(4):
                        ring[f"up{b}{j}"].taken(pe)
                    for i in range(HT):
                        for j in range(4):
                            ins = pe.matmul(s.ps[:, i * P:(i + 1) * P], up[:, j, HT * b + i], t["xa_w2"][:, j],
                                            start=(j == 0), stop=(j == 3), skip_group_check=True)
                    ins.then_inc(s.filled, 1)

                stages = {"film": film_of, "forth": forth, "back": back, "up": up_of, "down": down}
                for stage, b in order:
                    stages[stage](b)

            @block.scalar
            def _(act):
                step = core.steps(act, "act")
                load_exp_and_log(act)

                def move(name, dst, src=None):
                    s = ring[name]
                    s.ready(act)
                    act.copy(dst, s.ps[:, :] if src is None else src(s)).then_inc(s.drained, 1)

                core.norm.act(act, step)
                move("values", v[:, :, :], lambda s: s.ps[0:G, 0:B * P])
                for b in range(B):
                    move(f"xT{b}", xT[:, half(b)])
                    move(f"q{b}", qT[:, half(b)])
                core.norm.act(act, step)

                def exp(g):
                    act.wait_ge(shifted, g + 1)
                    act.activation(prob[:, g % 2], prob[:, g % 2], ACT.Exp).then_inc(exps, 1)

                def context(b):
                    move(f"meanT{b}", meanT[:, half(b)], lambda s: s.ps[0:G, :])
                    move(f"c{b}", cT[:, half(b)])

                def film_of(b):
                    for g in range(HT * b, HT * b + HT):
                        s = ring[f"film{g}"]
                        s.ready(act)
                        f = film[:, g].rearrange("p (o k) c -> p o k c", o=2)
                        p = s.ps[:, :].rearrange("p (o k c) -> p o k c", o=2, k=2)
                        gate = rows["mod_gate"]
                        act.activation(f[:, :, 0], p[:, :, 0], ACT.Identity, scale=gate,
                                       bias=1.0).then_inc(film_ready, 1)
                        act.activation(f[:, :, 1], p[:, :, 1], ACT.Copy, scale=gate).then_inc(s.drained, 1)

                def gelu(b):
                    for j in range(4):
                        s = ring[f"up{b}{j}"]
                        s.ready(act)
                        act.activation(up[:, j, half(b)], s.ps[:, :].rearrange("p (i t) -> p i t", i=HT), ACT.Gelu,
                                       bias=bias["xa_b1"][:, j:j + 1]).then_inc(s.drained, 1)

                exp(0)
                exp(1)
                move("taps", lags[:, :, :], lambda s: s.ps[:, :].rearrange("p (d b) -> p b d", b=LB))
                exp(2)
                exp(3)
                for name in ("kernel_re", "kernel_im"):
                    s = ring[name]
                    s.ready(act)
                    act.mul(t[name][:, :, :], s.ps[:, :].rearrange("p (f d) -> p f d", f=LT),
                            1.0 / T).then_inc(s.drained, 1)
                exp(4)
                context(0)
                exp(5)
                film_of(0)
                exp(6)
                exp(7)
                context(1)
                core.norm.act(act, step)
                film_of(1)
                move("hT0", hT[:, half(0)])
                core.norm.act(act, step)
                gelu(0)
                move("hT1", hT[:, half(1)])
                load_exp_and_log(act)
                core.norm.act(act, step)
                gelu(1)
                load_exp_and_log(act)
                for _ in range(2 * B - 1):
                    core.norm.act(act, step)
                core.keep("act", step)

            @block.gpsimd
            def _(pool):
                step = core.steps(pool, "pool")

                def weigh(g):
                    k = g % 2
                    pool.wait_ge(exps, g + 1)
                    step(pool.tensor_scalar(left[:, k], left[:, k], SELECTED, None, ALU.is_equal))
                    pool.tensor_tensor(prob[:, k], left[:, k], prob[:, k], ALU.mult).then_inc(weighed, 1)

                def average(g):
                    k = g % 2
                    pool.wait_ge(total_ready, g + 1)
                    step(pool.tensor_tensor(prob[:, k], prob[:, k], spread(total[:, k], 2, [P, H, G]), ALU.mult))
                    step(pool.tensor_tensor(prob[:, k, 0:2], prob[:, k, 0:2], prob[:, k, 2:4], ALU.add))
                    pool.tensor_tensor(mean[:, g], prob[:, k, 0], prob[:, k, 1], ALU.add).then_inc(mean_ready, 1)

                def modulate(b):
                    hb = half(b)
                    ring[f"film{HT * b + HT - 1}"].taken(pool)
                    pool.wait_ge(film_ready, HT * b + HT)
                    pool.wait_ge(normed, b + 1)
                    step(pool.tensor_tensor(u[:, hb], u[:, hb], film[:, hb, 0], ALU.mult))
                    pool.tensor_tensor(u[:, hb], u[:, hb], film[:, hb, 1], ALU.add).then_inc(u_ready, 1)
                    pool.wait_ge(u_ready, b + 1)
                    pool.tensor_tensor(xt[:, hb], u[:, hb], spread(rows["d_skip"], 1, [P, HT, P]),
                                       ALU.mult).then_inc(skip_ready, 1)

                def combine(b):
                    if b:
                        ring[f"y{b - 1}"].ready(pool)
                    pool.wait_ge(part_ready, 2 * b + 2)
                    pool.tensor_tensor(yr[:, :], part[0][:, :], part[1][:, :], ALU.subtract).then_inc(y_ready, 1)
                    ring[f"xr{b}"].taken(pool)
                    ring[f"xi{b}"].taken(pool)
                    pool.tensor_tensor(yi[:, :], part[2][:, :], part[3][:, :], ALU.add).then_inc(y_ready, 1)

                def add_bias(b):
                    pool.wait_ge(xt_ready, b + 1)
                    pool.tensor_tensor(u[:, half(b)], xt[:, half(b)], spread(rows["xa_b2"], 1, [P, HT, P]),
                                       ALU.add).then_inc(biased, 1)

                for g in range(NT):
                    weigh(g)
                    average(g)
                    if g == 5:
                        modulate(0)
                combine(0)
                modulate(1)
                add_bias(0)
                combine(1)
                for b in range(B):
                    pool.tensor_tensor(x_bias[:, half(b)], x[:, half(b)], spread(rows["b_out"], 1, [P, HT, P]),
                                       ALU.add).then_inc(x_bias_ready, 1)
                add_bias(1)
                core.keep("pool", step)

            @block.vector
            def _(dve):
                step = core.steps(dve, "dve")
                core.wait_loaded(dve, "xa")
                def norm_in(b):
                    core.norm.dve(dve, step, x[:, half(b)], u[:, half(b)])
                    step.wait()
                    step(dve.tensor_tensor(u[:, half(b)], u[:, half(b)], spread(rows["g_in"], 1, [P, HT, P]),
                                           ALU.mult))
                    dve.tensor_tensor(u[:, half(b)], u[:, half(b)], spread(rows["b_in"], 1, [P, HT, P]),
                                      ALU.add).then_inc(normed, 1)

                def select(g):
                    k = g % 2
                    s = ring[f"s{g}"]
                    s.ready(dve)
                    dve.tensor_tensor(score[:, k], s.ps[:, 0:H * G].rearrange("p (h g) -> p h g", h=H),
                                      spread(mask_bias[:, g // HT], 1, [P, H, G]), ALU.add).then_inc(s.drained, 1)
                    s.taken(dve)
                    for r in range(K_TOP // 8):
                        src = left if r else score
                        for hh in range(H):
                            if r:
                                dve.wait_ge(step.sem, step.n - (H - 1))
                            step.mark(dve.max(top[:, k, r, hh], src[:, k, hh]))
                        for hh in range(H):
                            dve.wait_ge(step.sem, step.n - (H - 1))
                            step.mark(dve.match_replace(left[:, k, hh], top[:, k, r, hh], src[:, k, hh], SELECTED))
                    step.wait()
                    if g >= 2:
                        dve.wait_ge(mean_ready, g - 1)
                    dve.tensor_tensor(prob[:, k], score[:, k], spread(top[:, k, 0, :, 0], 2, [P, H, G]),
                                      ALU.subtract).then_inc(shifted, 1)

                def invert(g):
                    k = g % 2
                    dve.wait_ge(weighed, g + 1)
                    step(dve.tensor_reduce(total[:, k], prob[:, k], AX.X, ALU.add))
                    step(dve.reciprocal(total[:, k], total[:, k]))
                    dve.tensor_scalar(total[:, k], total[:, k], text_weight[:, g:g + 1], None,
                                      ALU.mult).then_inc(total_ready, 1)

                def multiply(b):
                    kr, ki = t["kernel_re"], t["kernel_im"]
                    if b == 0:
                        ring["kernel_re"].taken(dve)
                        ring["kernel_im"].taken(dve)
                    xr, xi = ring[f"xr{b}"], ring[f"xi{b}"]
                    xr.ready(dve)
                    xi.ready(dve)
                    for n, (a, kk, sig) in enumerate(((xr, kr, part_ready), (xi, ki, part_ready),
                                                      (xr, ki, xr.drained), (xi, kr, xi.drained))):
                        if b and n % 2 == 0:
                            dve.wait_ge(y_ready, n // 2 + 1)
                        dve.tensor_tensor(part[n][:, :], a.ps[:, :].rearrange("p (f d) -> p f d", f=LT),
                                          kk[:, :, :], ALU.mult).then_inc(sig, 1)

                def modulate(b):
                    hb = half(b)
                    s = ring[f"y{b}"]
                    s.ready(dve)
                    dve.wait_ge(skip_ready, b + 1)
                    dve.tensor_tensor(xt[:, hb], s.ps[:, :].rearrange("p (i d) -> p i d", i=HT), xt[:, hb],
                                      ALU.add).then_inc(s.drained, 1)
                    s.taken(dve)
                    step(dve.tensor_tensor(xt[:, hb], xt[:, hb], film[:, hb, 2], ALU.mult))
                    step(dve.tensor_tensor(xt[:, hb], xt[:, hb], film[:, hb, 3], ALU.add))
                    dve.tensor_tensor(xt[:, hb], xt[:, hb], x[:, hb], ALU.add).then_inc(xt_ready, 1)
                    dve.wait_ge(xt_ready, b + 1)
                    core.norm.dve(dve, step, xt[:, hb], h[:, hb])
                    step.wait()
                    step(dve.tensor_tensor(h[:, hb], h[:, hb], spread(rows["g_ffn"], 1, [P, HT, P]), ALU.mult))
                    dve.tensor_tensor(h[:, hb], h[:, hb], spread(rows["b_ffn"], 1, [P, HT, P]),
                                      ALU.add).then_inc(h_ready, 1)

                def finish(b):
                    hb = half(b)
                    s = ring[f"down{b}"]
                    s.ready(dve)
                    dve.wait_ge(biased, b + 1)
                    dve.tensor_tensor(xt[:, hb], s.ps[:, :].rearrange("p (i c) -> p i c", i=HT), u[:, hb],
                                      ALU.add).then_inc(s.drained, 1)
                    s.taken(dve)
                    core.norm.dve(dve, step, xt[:, hb], xt[:, hb])
                    step.wait()
                    step(dve.tensor_tensor(xt[:, hb], xt[:, hb], spread(rows["g_out"], 1, [P, HT, P]), ALU.mult))
                    dve.wait_ge(x_bias_ready, b + 1)
                    step(dve.tensor_tensor(xt[:, hb], xt[:, hb], x_bias[:, hb], ALU.add))
                    core.norm.dve(dve, step, xt[:, hb], out[:, hb])

                norm_in(0)
                s = ring["keys"]
                s.ready(dve)
                for b in range(B):
                    dve.tensor_tensor(k_wide[:, b], spread(s.ps[:, b * G:(b + 1) * G], 1, [P, H, G]),
                                      spread(t["head4_of"][:, :], 2, [P, H, G]), ALU.mult
                                      ).then_inc(consts_ready if b else s.drained, 1)
                step(dve.tensor_copy(mask_bias[:, :, :], t["mask_ctx"][:, :, :]))
                dve.tensor_scalar(mask_bias[:, :, :], mask_bias[:, :, :], 1.0, -VERY_LOW, ALU.subtract,
                                  ALU.mult).then_inc(consts_ready, 1)
                step(dve.tensor_copy(text_weight[:, :], t["mask_text"][:, :]))
                dve.tensor_scalar(text_weight[:, :], text_weight[:, :], 1.0 / H, None,
                                  ALU.mult).then_inc(consts_ready, 1)
                dve.memset(ones[:, :], 1.0).then_inc(consts_ready, 1)
                dve.memset(total[:, :, :], 0.0).then_inc(consts_ready, 1)
                dve.wait_ge(consts_ready, 5)
                norm_in(1)
                select(0)
                for g in range(NT):
                    if g + 1 < NT:
                        select(g + 1)
                    invert(g)
                multiply(0)
                modulate(0)
                multiply(1)
                modulate(1)
                finish(0)
                finish(1)
                step.wait()
                core.keep("dve", step)



NE, HD = 16, 64


def expert_attention(core, x, out):
    nc = core.nc
    t = core.tiles
    with ExitStack() as ctx:
        def sb(name, shape, dt=F32):
            return core.tile("ea_" + name, shape, dt, ctx)

        def sem(name):
            return ctx.enter_context(nc.semaphore("ea_" + name))

        ident = t["ident"]
        rows = {n: t["rows"][:, a:b] for n, (a, b) in core.rows.items()}
        xT = sb("xT", [P, NT, P])
        square = sb("square", [P, NT, P])
        sim_square = sb("sim_square", [P, NE])
        ones = sb("ones", [P, P])
        sim_unit = sb("sim_unit", [P, NE])
        size = sb("size", [P, NT + NE])
        size_log = sb("size_log", [P, NT + NE])
        unit = sb("unit", [P, NT + NE])
        spare = sb("spare", [P, NT + NE])
        sigma = sb("sigma", [P, NE])
        logit = sb("logit", [P, NT, NE])
        gate = sb("gate", [P, NT, NE])
        chosen = sb("chosen", [P, NT, NE])
        second = sb("second", [P, NT, NE])
        best = sb("best", [P, NT, 8])
        few = sb("few", [P, NT])
        most = sb("most", [P, NT])
        parts = sb("parts", [P, NT, 3, NE], BF16)
        parts32 = sb("parts32", [P, NT, 3 * NE])
        gateT = sb("gateT", [3 * NE, NT, P], BF16)
        NX = 4
        xw = sb("xw", [P, NX, HT, P])
        qk_rows = sb("qk_rows", [P, NT, 2 * HD])
        qT, kT = sb("qT", [HD, NT, P]), sb("kT", [HD, NT, P])
        v2 = sb("v2", [P, NT, 2, HD])
        top = sb("top", [P, NT])
        total = sb("total", [P, NT])
        prob = sb("prob", [P, 2, HT * P])
        probT = sb("probT", [P, 2, HT, P])
        attT = sb("attT", [P, NT, P])
        mixed = sb("mixed", [P, NX, HT, P])
        res = sb("res", [P, NT, P])

        plan = ["size"]
        for b in range(B):
            plan += [f"xT{b}", f"logit{b}"]
        plan += [f"gateT{b}" for b in range(B)]
        for b in range(B):
            plan += [f"gate{b}_{e}" for e in range(NE)]
        for b in range(B):
            plan += [f"qkT{b}", f"s{b}0"]
            for i in range(HT):
                plan += ([f"s{b}{i + 1}"] if i + 1 < HT else []) + [f"pT{b}{i}"]
        for b in range(B):
            plan += [f"mix{b}_{j}" for j in range(NE // 2)]
        ring = core.ring.plan(plan, range(4, BANKS))
        held = core.ring.plan(["qkv00", "qkv01", "qkv10", "qkv11", "att0", "att1", "out0", "out1"], range(4))

        squares = sem("squares")
        sizes = sem("sizes")
        unit_log = sem("unit_log")
        sigma_exp = sem("sigma_exp")
        unit_ready = sem("unit_ready")
        shifted, exps = sem("shifted"), sem("exps")
        parts_ready = sem("parts_ready")
        used = sem("used")
        rows_ready, q_ready = sem("rows_ready"), sem("q_ready")
        max_ready, prob_ready = sem("max_ready"), sem("prob_ready")
        mixed_used = sem("mixed_used")

        def half(b):
            return slice(HT * b, HT * b + HT)

        with nc.Block() as block:
            @block.sync
            def _(sp):
                core.issue_loads(sp)

            @block.tensor
            def _(pe):
                core.wait_loaded(pe, "ea")
                s = ring["size"]
                s.claim(pe)
                pe.wait_ge(squares, 2)
                pe.matmul(s.ps[:, 0:NE], ones[:, :], sim_square[:, :], start=True, stop=True).then_inc(s.filled, 1)
                for b in range(B):
                    s = ring[f"xT{b}"]
                    s.claim(pe)
                    for i in range(HT):
                        ins = pe.transpose(s.ps[:, i * P:(i + 1) * P], x[:, HT * b + i], ident[:, :])
                    ins.then_inc(s.filled, 1)
                    s.taken(pe)
                    s = ring[f"logit{b}"]
                    s.claim(pe)
                    pe.wait_ge(unit_ready, 2)
                    for i in range(HT):
                        ins = pe.matmul(s.ps[:, i * NE:(i + 1) * NE], xT[:, HT * b + i], sim_unit[:, :], start=True,
                                        stop=True, skip_group_check=True)
                    ins.then_inc(s.filled, 1)
                for b in range(B):
                    s = ring[f"gateT{b}"]
                    s.claim(pe)
                    pe.wait_ge(parts_ready, 1)
                    for i in range(HT):
                        ins = pe.transpose(s.ps[0:3 * NE, i * P:(i + 1) * P], parts32[:, HT * b + i], ident[:, :])
                    ins.then_inc(s.filled, 1)

                LEAD = 3

                def spread_gate(b, e):
                    s = ring[f"gate{b}_{e}"]
                    s.claim(pe)
                    pe.matmul(s.ps[:, :], t["expert_row"][:, e], gateT[:, half(b)], start=True,
                              stop=True).then_inc(s.filled, 1)

                for b in range(B):
                    ring[f"gateT{b}"].taken(pe)
                    qkv = [held[f"qkv{b}{n}"] for n in range(2)]
                    for s in qkv:
                        s.claim(pe)
                    for e in range(LEAD):
                        spread_gate(b, e)
                    for e in range(NE):
                        if e + LEAD < NE:
                            spread_gate(b, e + LEAD)
                        n = NE * b + e
                        ring[f"gate{b}_{e}"].taken(pe)
                        for i in range(HT):
                            s = qkv[i // 2]
                            ins = pe.matmul(s.ps[:, i % 2 * 3 * HD:(i % 2 + 1) * 3 * HD], xw[:, n % NX, i],
                                            t["w_qkv"][:, e], start=(e == 0 and i % 2 == 0), stop=(e == NE - 1),
                                            skip_group_check=True)
                            if e == NE - 1 and i % 2:
                                ins.then_inc(s.filled, 1)
                        if e < NE - 1:
                            ins.then_inc(used, 1)
                for b in range(B):
                    s = ring[f"qkT{b}"]
                    s.claim(pe)
                    pe.wait_ge(rows_ready, 2 * b + 2)
                    for i in range(HT):
                        ins = pe.transpose(s.ps[:, i * P:(i + 1) * P], qk_rows[:, HT * b + i], ident[:, :])
                    ins.then_inc(s.filled, 1)
                    for s in (held[f"qkv{b}0"], held[f"qkv{b}1"], ring[f"qkT{b}"]):
                        s.taken(pe)
                    pe.wait_ge(q_ready, b + 1)

                    def attend(i):
                        s = ring[f"s{b}{i}"]
                        s.claim(pe)
                        pe.matmul(s.ps[:, 0:(i + 1) * P], qT[:, HT * b + i], kT[:, HT * b:HT * b + i + 1], start=True,
                                  stop=True).then_inc(s.filled, 1)

                    attend(0)
                    a = held[f"att{b}"]
                    for i in range(HT):
                        if i + 1 < HT:
                            attend(i + 1)
                        s = ring[f"pT{b}{i}"]
                        s.claim(pe)
                        pe.wait_ge(prob_ready, HT * b + i + 1)
                        for j in range(i + 1):
                            ins = pe.transpose(s.ps[:, j * P:(j + 1) * P], prob[:, i % 2, j * P:(j + 1) * P],
                                               ident[:, :])
                        ins.then_inc(s.filled, 1)
                        s.taken(pe)
                        if i == 0:
                            a.claim(pe)
                        for j in range(i + 1):
                            ins = pe.matmul(a.ps[:, i * P:(i + 1) * P], v2[:, HT * b + j], probT[:, i % 2, j],
                                            start=(j == 0), stop=(j == i), skip_group_check=True)
                    ins.then_inc(a.filled, 1)
                for b in range(B):
                    o = held[f"out{b}"]
                    o.claim(pe)
                    held[f"att{b}"].taken(pe)

                    def spread_pair(j):
                        s = ring[f"mix{b}_{j}"]
                        s.claim(pe)
                        pe.matmul(s.ps[:, :], t["expert_pair"][:, j], gateT[:, half(b)], start=True,
                                  stop=True).then_inc(s.filled, 1)

                    for j in range(LEAD):
                        spread_pair(j)
                    for j in range(NE // 2):
                        if j + LEAD < NE // 2:
                            spread_pair(j + LEAD)
                        n = NE // 2 * b + j
                        ring[f"mix{b}_{j}"].taken(pe)
                        for i in range(HT):
                            ins = pe.matmul(o.ps[:, i * P:(i + 1) * P], mixed[:, n % NX, i], t["w_o"][:, j],
                                            start=(j == 0 and i == 0), stop=(j == NE // 2 - 1),
                                            skip_group_check=True)
                        ins.then_inc(o.filled if j == NE // 2 - 1 else mixed_used, 1)

            @block.scalar
            def _(act):
                step = core.steps(act, "act")
                load_exp_and_log(act)
                act.activation(sigma[:, :], rows["gates"], ACT.Exp, scale=-1.0).then_inc(sigma_exp, 1)
                act.wait_ge(sizes, 1)
                step(act.activation(size_log[:, :], size[:, :], ACT.Ln, scale=float(2 ** 40)))
                act.activation(unit[:, :], size_log[:, :], ACT.Exp, scale=-0.5).then_inc(unit_log, 1)
                for b in range(B):
                    s = ring[f"xT{b}"]
                    s.ready(act)
                    act.copy(xT[:, half(b)], s.ps[:, :]).then_inc(s.drained, 1)
                act.wait_ge(shifted, 1)
                act.activation(gate[:, :, :], gate[:, :, :], ACT.Exp).then_inc(exps, 1)
                for b in range(B):
                    s = ring[f"gateT{b}"]
                    s.ready(act)
                    act.copy(gateT[:, half(b)], s.ps[0:3 * NE, :]).then_inc(s.drained, 1)
                for b in range(B):
                    for n in range(2):
                        s = held[f"qkv{b}{n}"]
                        s.ready(act)
                        g = HT * b + 2 * n
                        rows_of = s.ps[:, 0:6 * HD].rearrange("p (i n) -> p i n", i=2)
                        act.copy(qk_rows[:, g:g + 2], rows_of[:, :, 0:2 * HD]).then_inc(rows_ready, 1)
                        act.copy(v2[:, g:g + 2], spread(rows_of[:, :, 2 * HD:], 2, [P, 2, 2, HD])
                                 ).then_inc(s.drained, 1)
                for b in range(B):
                    s = ring[f"qkT{b}"]
                    s.ready(act)
                    act.mul(qT[:, half(b)], s.ps[0:HD, :], HD ** -0.5).then_inc(q_ready, 1)
                    act.copy(kT[:, half(b)], s.ps[HD:2 * HD, :]).then_inc(s.drained, 1)
                    for i in range(HT):
                        g = HT * b + i
                        s = ring[f"s{b}{i}"]
                        act.wait_ge(max_ready, g + 1)
                        if g >= 2:
                            last = ring[f"pT{(g - 2) // HT}{(g - 2) % HT}"]
                            last.ready(act)
                        act.activation(prob[:, g % 2, 0:(i + 1) * P], s.ps[:, 0:(i + 1) * P], ACT.Exp,
                                       bias=top[:, g:g + 1], accum_out=total[:, g:g + 1]).then_inc(s.drained, 1)
                        s = ring[f"pT{b}{i}"]
                        s.ready(act)
                        act.copy(probT[:, i % 2, 0:i + 1], s.ps[:, 0:(i + 1) * P].rearrange("p (j s) -> p j s", s=P)
                                 ).then_inc(s.drained, 1)
                    s = held[f"att{b}"]
                    s.ready(act)
                    act.copy(attT[:, half(b)], s.ps[:, :]).then_inc(s.drained, 1)
                for b in range(B):
                    core.norm.act(act, step)
                core.keep("act", step)

            @block.vector
            def _(dve):
                step = core.steps(dve, "dve")
                core.wait_loaded(dve, "ea")
                dve.memset(ones[:, :], 1.0).then_inc(squares, 1)
                dve.tensor_tensor(sim_square[:, :], t["sim"][:, :], t["sim"][:, :], ALU.mult).then_inc(squares, 1)
                step(dve.tensor_tensor(square[:, :, :], x[:, :, :], x[:, :, :], ALU.mult))
                step(dve.tensor_reduce(size[:, 0:NT], square[:, :, :], AX.X, ALU.add))
                s = ring["size"]
                s.ready(dve)
                dve.tensor_copy(size[:, NT:], s.ps[:, 0:NE]).then_inc(s.drained, 1)
                s.taken(dve)
                dve.tensor_scalar(size[:, :], size[:, :], 1e-24, None, ALU.max).then_inc(sizes, 1)
                dve.wait_ge(unit_log, 1)
                step(dve.tensor_scalar(unit[:, :], unit[:, :], float(2 ** 20), None, ALU.mult))
                step(dve.tensor_tensor(spare[:, :], unit[:, :], unit[:, :], ALU.mult))
                step(dve.scalar_tensor_tensor(spare[:, :], spare[:, :], -0.5, size[:, :], ALU.mult, ALU.mult))
                dve.scalar_tensor_tensor(unit[:, :], spare[:, :], 1.5, unit[:, :], ALU.add,
                                         ALU.mult).then_inc(unit_ready, 1)
                dve.wait_ge(unit_ready, 1)
                dve.tensor_tensor(sim_unit[:, :], t["sim"][:, :], unit[:, NT:], ALU.mult).then_inc(unit_ready, 1)
                dve.wait_ge(sigma_exp, 1)
                step(dve.tensor_scalar(sigma[:, :], sigma[:, :], 1.0, None, ALU.add))
                step(dve.reciprocal(sigma[:, :], sigma[:, :]))

                lg, gt, ch, se = logit[:, :], gate[:, :], chosen[:, :], second[:, :]
                cube = [P, NT, NE]
                for b in range(B):
                    s = ring[f"logit{b}"]
                    s.ready(dve)
                    dve.tensor_tensor(logit[:, half(b)], s.ps[:, 0:HT * NE].rearrange("p (i e) -> p i e", i=HT),
                                      spread(unit[:, half(b)], 2, [P, HT, NE]), ALU.mult).then_inc(s.drained, 1)
                for b in range(B):
                    ring[f"logit{b}"].taken(dve)
                step(dve.tensor_tensor(lg, lg, spread(sigma[:, :], 1, cube), ALU.subtract))
                for g in range(NT):
                    step.mark(dve.max(best[:, g], logit[:, g]))
                step.mark(dve.tensor_scalar(ch, lg, 0.0, None, ALU.is_gt))
                step.mark(dve.tensor_scalar(gt, lg, 0.0, None, ALU.max))
                step.wait()
                step.mark(dve.tensor_scalar(few[:, :], best[:, :, 0], 0.0, None, ALU.is_le))
                step.mark(dve.tensor_scalar(most[:, :], best[:, :, 0], 0.0, None, ALU.max))
                step(dve.memset(best[:, :, 2:8], SELECTED))
                dve.tensor_tensor(gt, gt, spread(most[:, :], 2, cube), ALU.subtract).then_inc(shifted, 1)
                for g in range(NT):
                    step.mark(dve.match_replace(second[:, g], best[:, g], logit[:, g], SELECTED))
                step.wait()
                step(dve.scalar_tensor_tensor(se, se, SELECTED, spread(few[:, :], 2, cube), ALU.is_equal, ALU.mult))
                step(dve.tensor_tensor(ch, ch, se, ALU.max))
                dve.wait_ge(exps, 1)
                step(dve.tensor_tensor(gt, gt, ch, ALU.mult))
                step(dve.tensor_reduce(most[:, :], gt, AX.X, ALU.add))
                step(dve.reciprocal(most[:, :], most[:, :]))
                step(dve.tensor_tensor(gt, gt, spread(most[:, :], 2, cube), ALU.mult))
                step(dve.tensor_copy(parts[:, :, 0], gt))
                step(dve.tensor_tensor(gt, gt, parts[:, :, 0], ALU.subtract))
                step(dve.tensor_copy(parts[:, :, 1], gt))
                step(dve.tensor_tensor(parts[:, :, 2], gt, parts[:, :, 1], ALU.subtract))
                dve.tensor_copy(parts32[:, :], parts[:, :].rearrange("p i a e -> p i (a e)")
                                ).then_inc(parts_ready, 1)
                for b in range(B):
                    for e in range(NE):
                        n = NE * b + e
                        s = ring[f"gate{b}_{e}"]
                        s.ready(dve)
                        if n >= NX:
                            m = n - NX
                            if m % NE == NE - 1:
                                held[f"qkv{m // NE}1"].ready(dve)
                            else:
                                dve.wait_ge(used, m + 1 - m // NE)
                        dve.tensor_tensor(xw[:, n % NX], xT[:, half(b)],
                                          s.ps[:, :].rearrange("p (i t) -> p i t", i=HT),
                                          ALU.mult).then_inc(s.drained, 1)
                for b in range(B):
                    for i in range(HT):
                        g = HT * b + i
                        s = ring[f"s{b}{i}"]
                        s.ready(dve)
                        diag = s.ps[:, i * P:(i + 1) * P]
                        step(dve.tensor_tensor(diag, diag, t["causal_bias"][:, :], ALU.add))
                        dve.tensor_reduce(top[:, g:g + 1], s.ps[:, 0:(i + 1) * P], AX.X, ALU.max,
                                          negate=True).then_inc(max_ready, 1)
                        s.taken(dve)
                        step(dve.reciprocal(total[:, g:g + 1], total[:, g:g + 1]))
                        dve.tensor_scalar(prob[:, g % 2, 0:(i + 1) * P], prob[:, g % 2, 0:(i + 1) * P],
                                          total[:, g:g + 1], None, ALU.mult).then_inc(prob_ready, 1)
                for b in range(B):
                    held[f"att{b}"].taken(dve)
                    for j in range(NE // 2):
                        n = NE // 2 * b + j
                        s = ring[f"mix{b}_{j}"]
                        s.ready(dve)
                        if n >= NX:
                            m = n - NX
                            if m % (NE // 2) == NE // 2 - 1:
                                held[f"out{m // (NE // 2)}"].ready(dve)
                            else:
                                dve.wait_ge(mixed_used, m + 1 - m // (NE // 2))
                        dve.tensor_tensor(mixed[:, n % NX], attT[:, half(b)],
                                          s.ps[:, :].rearrange("p (i t) -> p i t", i=HT),
                                          ALU.mult).then_inc(s.drained, 1)
                    s = held[f"out{b}"]
                    s.ready(dve)
                    dve.tensor_tensor(res[:, half(b)], s.ps[:, :].rearrange("p (i c) -> p i c", i=HT), x[:, half(b)],
                                      ALU.add).then_inc(s.drained, 1)
                    s.taken(dve)
                    core.norm.dve(dve, step, res[:, half(b)], out[:, half(b)])
                step.wait()
                core.keep("dve", step)



NH, HC, HV = 8, 64, 128
NP = NH // 2
BLK = 32
NB = P // BLK
RANGE = 80.0
BEFORE, WHOLE, AFTER, OWN, NSC = 0, NB, NB + 1, 2 * NB + 1, 3 * NB + 1


def gated_attention(core, x, out):
    nc = core.nc
    t = core.tiles
    with ExitStack() as ctx:
        def sb(name, shape, dt=F32):
            return core.tile("ga_" + name, shape, dt, ctx)

        def sem(name):
            return ctx.enter_context(nc.semaphore("ga_" + name))

        ident = t["ident"]
        rows = {n: t["rows"][:, a:b] for n, (a, b) in core.rows.items()}
        xn = sb("xn", [P, NT, P])
        xT = sb("xT", [P, NT, P])
        qvT = sb("qvT", [P, NT, P])
        kT = sb("kT", [P, NT, P])
        k_square = sb("k_square", [P, NT, P])
        k_size = sb("k_size", [P, NT, P])
        k_root = sb("k_root", [P, NT, P])
        ones = sb("ones", [P, P])

        def two(name, *shape):
            return sb(name, [P, 2, *shape])

        soft = two("soft", NP, P)
        cum = two("cum", NP, P)
        to_mid, to_end = two("to_mid", NP, P), two("to_end", NP, P)
        q = two("q", NP, P)
        q_mid, k_mid = two("q_mid", NP, P), two("k_mid", NP, P)
        q_in, k_in = two("q_in", NP, P), two("k_in", NP, P)
        q_two, k_two = two("q_two", NP, 2, BLK), two("k_two", NP, 2, BLK)
        q_all, k_all = two("q_all", NP, P), two("k_all", NP, P)
        scale_log, scale = two("scale_log", NP, NSC), sb("scale", [P, 3, NP, NSC])
        v = two("v", NH, HV)
        k_rows = two("k_rows", NP, P)
        scores = two("scores", 2, NP, P)
        vw = sb("vw", [P, NH, P])
        minus_bias = sb("minus_bias", [P, NP])
        state = two("state", NP, HV)
        res = sb("res", [P, NT, P])

        plan = ["vw0", "vw1"]
        for b in range(B):
            plan += [f"xT{b}", f"qv{b}", f"k{b}"]

        def order():
            out = [("front", 0), ("front", 1), ("size", 0), ("size", 1), ("mid", 0)]
            for g in range(NT):
                out += [("front", g + 2)] if g + 2 < NT else []
                out += [("mid", g + 1)] if g + 1 < NT else []
                out += [("back", g)]
            return out

        stage_banks = {"front": ["z", "q"], "mid": ["v0", "v1", "s0", "s1", "kt"], "back": ["y", "st"]}
        stage_banks["size"] = ["ksize"]
        for stage, g in order():
            plan += [f"{n}_{g}" for n in stage_banks[stage] if not (n == "st" and g % HT == HT - 1)]
        ring = core.ring.plan(plan, range(BANKS))

        xn_ready = sem("xn_ready")
        ones_ready = sem("ones_ready")
        bias_ready = sem("bias_ready")
        soft_parts = sem("soft_parts")
        square_ready = sem("square_ready")
        k_root_ready, k_ready = sem("k_root_ready"), sem("k_ready")
        soft_capped, soft_ready = sem("soft_capped"), sem("soft_ready")
        cum_ready = sem("cum_ready")
        logs_ready = sem("logs_ready")
        mid_ready = sem("mid_ready")
        exps = sem("exps")
        products = sem("products")
        copies = sem("copies")
        zeroed = sem("zeroed")

        def half(b):
            return slice(HT * b, HT * b + HT)

        def blocks(ap):
            return ap.rearrange("p h (n c) -> p h n c", c=BLK)

        with nc.Block() as block:
            @block.sync
            def _(sp):
                core.issue_loads(sp)

            @block.tensor
            def _(pe):
                core.wait_loaded(pe, "ga")
                for n in range(2):
                    s = ring[f"vw{n}"]
                    s.claim(pe)
                    for i in range(4):
                        ins = pe.matmul(s.ps[HC:2 * HC, i * P:(i + 1) * P], t["ga_vcT"][:, 4 * n + i],
                                        t["ga_wo"][:, 4 * n + i], start=True, stop=True, skip_group_check=True)
                    ins.then_inc(s.filled, 1)
                pe.wait_ge(ones_ready, 1)
                for b in range(B):
                    s = ring[f"xT{b}"]
                    s.claim(pe)
                    pe.wait_ge(xn_ready, b + 1)
                    for i in range(HT):
                        ins = pe.transpose(s.ps[:, i * P:(i + 1) * P], xn[:, HT * b + i], ident[:, :])
                    ins.then_inc(s.filled, 1)
                    s.taken(pe)
                    for name, w in ((f"qv{b}", t["ga_wqv"]), (f"k{b}", t["ga_wkk"])):
                        s = ring[name]
                        s.claim(pe)
                        pe.matmul(s.ps[:, :], w[:, :], xT[:, half(b)], start=True, stop=True).then_inc(s.filled, 1)

                def size(b):
                    s = ring[f"ksize_{b}"]
                    s.claim(pe)
                    pe.wait_ge(square_ready, b + 1)
                    pe.matmul(s.ps[:, :], ones[0:HC, :], k_square[0:HC, half(b)], start=True,
                              stop=True).then_inc(s.filled, 1)

                def front(g):
                    s = ring[f"z_{g}"]
                    s.claim(pe)
                    for p in range(NP):
                        cols = slice(p * P, (p + 1) * P)
                        ins = pe.matmul(s.ps[:, cols], t["ga_wa"][:, cols], xT[:, g], start=True, stop=True,
                                        skip_group_check=True)
                    ins.then_inc(s.filled, 1)
                    ring[f"qv{g // HT}"].taken(pe)
                    s = ring[f"q_{g}"]
                    s.claim(pe)
                    for p in range(NP):
                        ins = pe.matmul(s.ps[:, p * P:(p + 1) * P], t["ga_qc"][:, p], qvT[0:HC, g], start=True,
                                        stop=True, skip_group_check=True)
                    ins.then_inc(s.filled, 1)

                def mid(g):
                    k = g % 2
                    for n in range(2):
                        s = ring[f"v{n}_{g}"]
                        s.claim(pe)
                        if g == 0:
                            ring[f"vw{n}"].taken(pe)
                        pe.matmul(s.ps[:, :], qvT[HC:2 * HC, g], vw[HC:2 * HC, 4 * n:4 * n + 4],
                                  start=True, stop=True).then_inc(s.filled, 1)
                    pe.wait_ge(products, 8 * g + 7)
                    pe.wait_ge(copies, 2 * (g + 1))
                    for n in range(2):
                        s = ring[f"s{n}_{g}"]
                        s.claim(pe)
                        own = slice(HC * n, HC * n + HC)
                        for p in range(NP):
                            out_ = s.ps[:, p * P:(p + 1) * P]
                            pe.matmul(out_, k_mid[own, k, p], q_mid[own, k, p], start=True, stop=True,
                                      skip_group_check=True)
                            for e in (0, 2):
                                pe.matmul(out_[e * BLK:(e + 1) * BLK, (e + 1) * BLK:(e + 2) * BLK],
                                          k_in[own, k, p, e * BLK:(e + 1) * BLK],
                                          q_in[own, k, p, (e + 1) * BLK:(e + 2) * BLK], start=True, stop=True,
                                          skip_group_check=True)
                            ins = pe.matmul(out_[0:2 * BLK, 2 * BLK:P], k_two[own, k, p], q_two[own, k, p],
                                            start=True, stop=True, skip_group_check=True)
                        ins.then_inc(s.filled, 1)
                    s = ring[f"kt_{g}"]
                    s.claim(pe)
                    for p in range(NP):
                        ins = pe.transpose(s.ps[:, p * P:(p + 1) * P], k_all[:, k, p], ident[:, :])
                    ins.then_inc(s.filled, 1)

                def back(g):
                    k = g % 2
                    first, last = g % HT == 0, g % HT == HT - 1
                    ring[f"v1_{g}"].taken(pe)
                    ring[f"kt_{g}"].taken(pe)
                    if not first:
                        ring[f"st_{g - 1}"].taken(pe)
                    s = ring[f"y_{g}"]
                    s.claim(pe)
                    pe.wait_ge(products, 8 * (g + 1))
                    if not first:
                        for p in range(NP):
                            pe.matmul(s.ps[:, 0:P], q_all[:, k, p], state[:, k, p], start=(p == 0), stop=False)
                    for n in range(2):
                        ring[f"s{n}_{g}"].taken(pe)
                        for p in range(NP):
                            ins = pe.matmul(s.ps[:, 0:P], scores[:, k, n, p], v[:, k, 2 * p + n],
                                            start=(first and n == 0 and p == 0), stop=(n == 1 and p == NP - 1))
                    ins.then_inc(s.filled, 1)
                    if not last:
                        s = ring[f"st_{g}"]
                        s.claim(pe)
                        for p in range(NP):
                            for n in range(2):
                                ins = pe.matmul(s.ps[HC * n:HC * n + HC, p * P:(p + 1) * P],
                                                k_rows[:, k, p, HC * n:HC * n + HC], v[:, k, 2 * p + n], start=True,
                                                stop=True, skip_group_check=True)
                        ins.then_inc(s.filled, 1)

                stages = {"size": size, "front": front, "mid": mid, "back": back}
                for stage, g in order():
                    stages[stage](g)

            @block.scalar
            def _(act):
                step = core.steps(act, "act")
                load_exp_and_log(act)
                for n in range(2):
                    s = ring[f"vw{n}"]
                    s.ready(act)
                    act.copy(vw[HC:2 * HC, 4 * n:4 * n + 4], s.ps[HC:2 * HC, :]).then_inc(s.drained, 1)
                act.mul(minus_bias[:, :], t["cols"][:, core.cols["wa_b"][0]:core.cols["wa_b"][1]],
                        -1.0).then_inc(bias_ready, 1)
                for b in range(B):
                    core.norm.act(act, step)
                act.wait_ge(bias_ready, 1)
                for b in range(B):
                    for name, dst in ((f"xT{b}", xT), (f"qv{b}", qvT), (f"k{b}", kT)):
                        s = ring[name]
                        s.ready(act)
                        act.copy(dst[:, half(b)], s.ps[:, :]).then_inc(s.drained, 1)

                def roots(b):
                    ring[f"ksize_{b}"].taken(act)
                    step(act.activation(k_root[:, half(b)], k_size[:, half(b)], ACT.Ln, scale=float(2 ** 40)))
                    act.activation(k_root[:, half(b)], k_root[:, half(b)], ACT.Exp, scale=-0.5
                                   ).then_inc(k_root_ready, 1)

                def front(g):
                    k = g % 2
                    s = ring[f"z_{g}"]
                    s.ready(act)
                    if g >= 2:
                        act.wait_ge(cum_ready, g - 1)
                    for p in range(NP):
                        act.activation(soft[:, k, p], s.ps[:, p * P:(p + 1) * P], ACT.Exp, scale=-1.0,
                                       bias=minus_bias[:, p:p + 1]).then_inc(soft_parts if p < NP - 1 else s.drained, 1)
                    s = ring[f"q_{g}"]
                    s.ready(act)
                    if g >= 2:
                        ring[f"s1_{g - 2}"].ready(act)
                    act.copy(q[:, k], s.ps[:, :]).then_inc(s.drained, 1)
                    act.wait_ge(soft_capped, g + 1)
                    act.activation(soft[:, k], soft[:, k], ACT.Ln, bias=1.0).then_inc(soft_ready, 1)

                def decays(g):
                    k = g % 2
                    act.wait_ge(mid_ready, g + 1)
                    act.wait_ge(logs_ready, 2 * (g + 1))
                    if g >= 2:
                        ring[f"s1_{g - 2}"].ready(act)
                        act.wait_ge(products, 8 * (g - 1))
                    if g >= 3 and (g - 3) % HT < HT - 1:
                        ring[f"st_{g - 3}"].taken(act)
                    for dst, src, sign in ((q_mid, to_mid, 1.0), (k_mid, to_mid, -1.0), (q_in, cum, 1.0),
                                           (k_in, to_end, -1.0)):
                        act.activation(dst[:, k], src[:, k], ACT.Exp, scale=sign).then_inc(exps, 1)
                    act.activation(scale[:, g % 3], scale_log[:, k], ACT.Exp).then_inc(exps, 1)

                def mid(g):
                    k = g % 2
                    if g >= 2:
                        m = g - 2
                        last = ring[f"st_{m}"] if m % HT < HT - 1 else ring[f"y_{m}"]
                        last.ready(act)
                    for n in range(2):
                        s = ring[f"v{n}_{g}"]
                        s.ready(act)
                        act.copy(v[:, k, 4 * n:4 * n + 4], s.ps[:, :]).then_inc(s.drained, 1)
                    ring[f"v0_{g}"].taken(act)
                    s = ring[f"kt_{g}"]
                    s.ready(act)
                    act.copy(k_rows[:, k], s.ps[:, :]).then_inc(s.drained, 1)

                front(0)
                front(1)
                for b in range(B):
                    roots(b)
                decays(0)
                decays(1)
                mid(0)
                for g in range(NT):
                    if g + 2 < NT:
                        front(g + 2)
                    if g + 1 < NT:
                        mid(g + 1)
                    if g + 2 < NT:
                        decays(g + 2)
                    if g in (HT + 1, NT - 1):
                        core.norm.act(act, step)
                core.keep("act", step)

            @block.gpsimd
            def _(pool):
                step = core.steps(pool, "pool")
                pool.memset(ones[:, :], 1.0).then_inc(ones_ready, 1)
                pool.memset(scores[:, :, :, :, :], 0.0).then_inc(zeroed, 1)
                pool.memset(scale_log[:, :, :, 0], 0.0).then_inc(zeroed, 1)

                def cap(g):
                    pool.wait_ge(soft_parts, (NP - 1) * (g + 1))
                    ring[f"z_{g}"].taken(pool)
                    pool.tensor_scalar(soft[:, g % 2], soft[:, g % 2], 1e19, None, ALU.min).then_inc(soft_capped, 1)

                def logs(g):
                    k = g % 2
                    pool.wait_ge(cum_ready, g + 1)
                    if g >= 2:
                        pool.wait_ge(exps, 5 * (g - 1))
                    if g == 0:
                        pool.wait_ge(zeroed, 2)
                    c = blocks(cum[:, k]).rearrange("p h n c -> p (h n) c")
                    shape = [P, NP * NB, BLK]
                    e = to_end[:, k].rearrange("p h (n c) -> p (h n) c", c=BLK)
                    pool.tensor_tensor(e, c, spread(c[:, :, BLK - 1], 2, shape), ALU.subtract).then_inc(logs_ready, 1)
                    sl = scale_log[:, k]
                    own = blocks(cum[:, k])[:, :, :, BLK - 1]
                    step.mark(pool.tensor_copy(sl[:, :, OWN:OWN + NB], own))
                    step(pool.tensor_copy(sl[:, :, BEFORE + 1], own[:, :, 0]))
                    for j in range(1, NB):
                        step(pool.tensor_tensor(sl[:, :, BEFORE + j + 1], sl[:, :, BEFORE + j], own[:, :, j],
                                                ALU.add))
                    pool.tensor_tensor(sl[:, :, AFTER:AFTER + NB], spread(sl[:, :, WHOLE], 2, [P, NP, NB]),
                                       sl[:, :, BEFORE + 1:WHOLE + 1], ALU.subtract).then_inc(logs_ready, 1)

                def copy(g):
                    k = g % 2
                    pool.wait_ge(products, 8 * g + 4)
                    pool.tensor_copy(k_two[:, k, :, 1], k_in[:, k, :, BLK:2 * BLK]).then_inc(copies, 1)
                    pool.tensor_copy(q_two[:, k, :, 0], q_in[:, k, :, 2 * BLK:3 * BLK]).then_inc(copies, 1)

                for g in range(2):
                    cap(g)
                for g in range(2):
                    logs(g)
                for g in range(2):
                    copy(g)
                for g in range(2, NT):
                    cap(g)
                    logs(g)
                    copy(g)
                core.keep("pool", step)

            @block.vector
            def _(dve):
                step = core.steps(dve, "dve")
                core.wait_loaded(dve, "ga")
                for b in range(B):
                    hb = half(b)
                    core.norm.dve(dve, step, x[:, hb], xn[:, hb])
                    step.wait()
                    step(dve.tensor_tensor(xn[:, hb], xn[:, hb], spread(rows["gamma"], 1, [P, HT, P]), ALU.mult))
                    dve.tensor_tensor(xn[:, hb], xn[:, hb], spread(rows["beta"], 1, [P, HT, P]),
                                      ALU.add).then_inc(xn_ready, 1)
                for b in range(B):
                    hb = half(b)
                    ring[f"k{b}"].taken(dve)
                    dve.tensor_tensor(k_square[:, hb], kT[:, hb], kT[:, hb], ALU.mult).then_inc(square_ready, 1)

                def size(b):
                    hb = half(b)
                    s = ring[f"ksize_{b}"]
                    s.ready(dve)
                    dve.tensor_scalar(k_size[:, hb], s.ps[:, :].rearrange("p (i c) -> p i c", i=HT), 1e-24, None,
                                      ALU.max).then_inc(s.drained, 1)

                def unit(b):
                    hb = half(b)
                    dve.wait_ge(k_root_ready, b + 1)
                    dve.scalar_tensor_tensor(kT[:, hb], k_root[:, hb], float(2 ** 20), kT[:, hb], ALU.mult,
                                             ALU.mult).then_inc(k_ready, 1)

                def scan(g):
                    k = g % 2
                    dve.wait_ge(soft_ready, g + 1)
                    if g >= 2:
                        dve.wait_ge(exps, 5 * (g - 1))
                    flat = "p h c -> p (h c)"
                    dve.tensor_tensor_scan(cum[:, k].rearrange(flat), t["restart"][:, :], soft[:, k].rearrange(flat),
                                           0.0, ALU.mult, ALU.subtract).then_inc(cum_ready, 1)
                    dve.wait_ge(cum_ready, g + 1)
                    c = blocks(cum[:, k]).rearrange("p h n c -> p (h n) c")
                    m = to_mid[:, k].rearrange("p h (n c) -> p (h n) c", c=BLK)
                    step(dve.tensor_tensor(m, c, spread(c[:, :, BLK // 2 - 1], 2, [P, NP * NB, BLK]), ALU.subtract))
                    dve.tensor_scalar(m, m, -RANGE, RANGE, ALU.max, ALU.min).then_inc(mid_ready, 1)

                def decay(g):
                    k = g % 2
                    if g % HT == 0:
                        dve.wait_ge(k_ready, g // HT + 1)
                    ring[f"q_{g}"].taken(dve)
                    kn = spread(kT[:, g], 1, [P, NP, P])
                    for n, (dst, src) in enumerate(((q_in, q[:, k]), (k_in, kn), (q_mid, q[:, k]), (k_mid, kn))):
                        dve.wait_ge(exps, 5 * g + (3, 4, 1, 2)[n])
                        dve.tensor_tensor(dst[:, k], dst[:, k], src, ALU.mult).then_inc(products, 1)
                    dve.wait_ge(exps, 5 * g + 5)
                    dve.wait_ge(products, 8 * g + 2)
                    if g >= 2:
                        ring[f"kt_{g - 2}"].ready(dve)
                    shape = [P, NP, NB, BLK]
                    sc = scale[:, g % 3]
                    dve.tensor_tensor(blocks(k_all[:, k]), blocks(k_in[:, k]),
                                      spread(sc[:, :, AFTER:AFTER + NB], 3, shape), ALU.mult).then_inc(products, 1)
                    dve.tensor_tensor(k_two[:, k, :, 0], k_in[:, k, :, 0:BLK],
                                      spread(sc[:, :, OWN + 1], 2, [P, NP, BLK]), ALU.mult).then_inc(products, 1)
                    dve.tensor_tensor(q_two[:, k, :, 1], q_in[:, k, :, 3 * BLK:],
                                      spread(sc[:, :, OWN + 2], 2, [P, NP, BLK]), ALU.mult).then_inc(products, 1)

                def decay_all(g):
                    k = g % 2
                    if g >= 2:
                        ring[f"y_{g - 2}"].ready(dve)
                    dve.tensor_tensor(blocks(q_all[:, k]), blocks(q_in[:, k]),
                                      spread(scale[:, g % 3, :, BEFORE:BEFORE + NB], 3, [P, NP, NB, BLK]),
                                      ALU.mult).then_inc(products, 1)

                def mid(g):
                    if g == 0:
                        dve.wait_ge(zeroed, 1)
                    if g >= 2:
                        ring[f"y_{g - 2}"].ready(dve)
                    for n in range(2):
                        s = ring[f"s{n}_{g}"]
                        s.ready(dve)
                        dve.copy_predicated(scores[:, g % 2, n], t["causal_bits"][:, :, :],
                                            s.ps[:, :].rearrange("p (h c) -> p h c", h=NP)).then_inc(s.drained, 1)

                def back(g):
                    if g % HT == HT - 1:
                        return
                    s = ring[f"st_{g}"]
                    s.ready(dve)
                    old, new = state[:, g % 2], state[:, (g + 1) % 2]
                    if g % HT == 0:
                        dve.tensor_copy(new, s.ps[:, :].rearrange("p (h c) -> p h c", h=NP)).then_inc(s.drained, 1)
                    else:
                        for p in range(NP):
                            ins = dve.scalar_tensor_tensor(new[:, p], old[:, p], scale[:, g % 3, p, WHOLE:WHOLE + 1],
                                                           s.ps[:, p * P:(p + 1) * P], ALU.mult, ALU.add)
                            if p < NP - 1:
                                step.mark(ins)
                            else:
                                ins.then_inc(s.drained, 1)
                    s.taken(dve)

                def last(g):
                    s = ring[f"y_{g}"]
                    s.ready(dve)
                    dve.scalar_tensor_tensor(res[:, g], x[:, g], 2.0, s.ps[:, 0:P], ALU.mult,
                                             ALU.add).then_inc(s.drained, 1)
                    s.taken(dve)

                scan(0)
                for b in range(B):
                    size(b)
                scan(1)
                for b in range(B):
                    unit(b)
                for g in range(2):
                    decay(g)
                    decay_all(g)
                mid(0)
                for g in range(NT):
                    if g + 2 < NT:
                        scan(g + 2)
                    if g + 1 < NT:
                        mid(g + 1)
                    if g + 2 < NT:
                        decay(g + 2)
                    back(g)
                    if g + 2 < NT:
                        decay_all(g + 2)
                    last(g)
                    if g in (HT + 1, NT - 1):
                        hb = half(g // (NT - 1))
                        core.norm.dve(dve, step, res[:, hb], out[:, hb])
                step.wait()
                core.keep("dve", step)



def cross_attention(core, x, out):
    nc = core.nc
    t = core.tiles
    H, D = 16, C // 16
    E = D + 1
    CLAMP = 10000.0
    PARTS = [(0, 6), (6, 12), (12, 16)]
    with ExitStack() as ctx:
        def sb(name, shape, dt=F32):
            return core.tile("ca_" + name, shape, dt, ctx)

        def sem(name):
            return ctx.enter_context(nc.semaphore("ca_" + name))

        ident = t["ident"]
        rows = {n: t["rows"][:, a:b] for n, (a, b) in core.rows.items()}
        bias = {n: t["cols"][:, a:b] for n, (a, b) in core.cols.items()}
        xT = sb("xT", [P, NT, P])
        qT = sb("qT", [P, NT, P])
        keys = sb("keys", [P, B, G])
        k_wide = sb("k_wide", [P, B, H, G])
        v_one = sb("v_one", [G, B, H, E])
        prob = sb("prob", [P, 2, H, G])
        most = sb("most", [P, 2, H])
        probT = sb("probT", [G, 2, H, P])
        den = sb("den", [P, 2, H])
        y = sb("y", [P, 2, P])
        yT = sb("yT", [P, 2, P])
        x_bias = sb("x_bias", [P, NT, P])
        res = sb("res", [P, NT, P])

        def order():
            out = [("score", 0), ("score", 1), ("turn", 0)]
            for g in range(NT):
                out += [("score", g + 2)] if g + 2 < NT else []
                out += [("turn", g + 1)] if g + 1 < NT else []
                out += [("sum", g)]
                out += [("project", g - 1)] if g else []
            return out + [("project", NT - 1)]

        stage_banks = {"score": ["s0", "s1", "s2"], "turn": ["t0", "t1", "t2", "t3"], "sum": ["o"],
                       "project": ["yT", "w"]}
        plan = ["keys", "values", "xT0", "q0", "xT1", "q1"]
        for stage, g in order():
            plan += [f"{n}_{g}" for n in stage_banks[stage]]
        ring = core.ring.plan(plan, range(BANKS))

        core.split_ready = core.sem("split_ready")
        high_ready = sem("high_ready")
        ones_ready = sem("ones_ready")
        wide_ready = sem("wide_ready")
        shifted, exps = sem("shifted"), sem("exps")
        x_bias_ready = sem("x_bias_ready")

        def half(b):
            return slice(HT * b, HT * b + HT)

        with nc.Block() as block:
            @block.sync
            def _(sp):
                core.issue_loads(sp)

            @block.tensor
            def _(pe):
                core.wait_loaded(pe, "ca")
                s = ring["keys"]
                s.claim(pe)
                pe.matmul(s.ps[:, 0:B * G], t["ca_wk"][:, :], t["ctxT"][:, :, :], start=True,
                          stop=True).then_inc(s.filled, 1)
                s = ring["values"]
                s.claim(pe)
                for b in range(B):
                    ins = pe.matmul(s.ps[0:G, b * P:(b + 1) * P], t["ctxT"][:, b], t["ca_wv"][:, :], start=True,
                                    stop=True, skip_group_check=True)
                ins.then_inc(s.filled, 1)
                for b in range(B):
                    s = ring[f"xT{b}"]
                    s.claim(pe)
                    for i in range(HT):
                        ins = pe.transpose(s.ps[:, i * P:(i + 1) * P], x[:, HT * b + i], ident[:, :])
                    ins.then_inc(s.filled, 1)
                    s.taken(pe)
                    s = ring[f"q{b}"]
                    s.claim(pe)
                    pe.matmul(s.ps[:, :], t["ca_wq"][:, :], xT[:, half(b)], start=True,
                              stop=True).then_inc(s.filled, 1)

                def score(g):
                    ring[f"q{g // HT}"].taken(pe)
                    pe.wait_ge(wide_ready, g // HT + 1)
                    for n, (lo, hi) in enumerate(PARTS):
                        s = ring[f"s{n}_{g}"]
                        s.claim(pe)
                        pe.matmul(s.ps[:, 0:(hi - lo) * G], qT[:, g], k_wide[:, g // HT, lo:hi], start=True,
                                  stop=True).then_inc(s.filled, 1)

                def turn(g):
                    pe.wait_ge(exps, g + 1)
                    for n in range(4):
                        s = ring[f"t{n}_{g}"]
                        s.claim(pe)
                        for i in range(4):
                            ins = pe.transpose(s.ps[0:G, i * P:(i + 1) * P], prob[:, g % 2, 4 * n + i], ident[:, :])
                        ins.then_inc(s.filled, 1)

                def total(g):
                    s = ring[f"o_{g}"]
                    s.claim(pe)
                    if g == 0:
                        pe.wait_ge(ones_ready, 1)
                        ring["values"].taken(pe)
                    for h in range(H):
                        if h % 4 == 0:
                            ring[f"t{h // 4}_{g}"].taken(pe)
                        ins = pe.matmul(s.ps[:, h * E:(h + 1) * E], probT[:, g % 2, h], v_one[:, g // HT, h],
                                        start=True, stop=True, skip_group_check=True)
                    ins.then_inc(s.filled, 1)

                def project(g):
                    ring[f"o_{g}"].taken(pe)
                    s = ring[f"yT_{g}"]
                    s.claim(pe)
                    pe.transpose(s.ps[:, 0:P], y[:, g % 2], ident[:, :]).then_inc(s.filled, 1)
                    s.taken(pe)
                    s = ring[f"w_{g}"]
                    s.claim(pe)
                    pe.matmul(s.ps[:, 0:P], yT[:, g % 2], t["ca_wo"][:, :], start=True, stop=True).then_inc(s.filled, 1)

                stages = {"score": score, "turn": turn, "sum": total, "project": project}
                for stage, g in order():
                    stages[stage](g)

            @block.scalar
            def _(act):
                step = core.steps(act, "act")
                load_exp_and_log(act)
                for b in range(B):
                    s = ring[f"xT{b}"]
                    s.ready(act)
                    act.copy(xT[:, half(b)], s.ps[:, :]).then_inc(s.drained, 1)
                    s = ring[f"q{b}"]
                    s.ready(act)
                    act.activation(qT[:, half(b)], s.ps[:, :].rearrange("p (i t) -> p i t", i=HT), ACT.Identity,
                                   bias=bias["bq"]).then_inc(s.drained, 1)

                def exp(g):
                    act.wait_ge(shifted, g + 1)
                    act.activation(prob[:, g % 2], prob[:, g % 2], ACT.Exp).then_inc(exps, 1)

                def turn(g):
                    if g >= 2:
                        ring[f"o_{g - 2}"].ready(act)
                    for n in range(4):
                        s = ring[f"t{n}_{g}"]
                        s.ready(act)
                        act.copy(probT[:, g % 2, 4 * n:4 * n + 4], s.ps[0:G, :]).then_inc(s.drained, 1)

                exp(0)
                exp(1)
                turn(0)
                for g in range(NT):
                    if g + 1 < NT:
                        turn(g + 1)
                    if g:
                        s = ring[f"yT_{g - 1}"]
                        s.ready(act)
                        act.copy(yT[:, (g - 1) % 2], s.ps[:, 0:P]).then_inc(s.drained, 1)
                    if g + 2 < NT:
                        exp(g + 2)
                    if g == HT:
                        core.norm.act(act, step)
                s = ring[f"yT_{NT - 1}"]
                s.ready(act)
                act.copy(yT[:, (NT - 1) % 2], s.ps[:, 0:P]).then_inc(s.drained, 1)
                core.norm.act(act, step)
                core.keep("act", step)

            @block.gpsimd
            def _(pool):
                pool.memset(v_one[:, :, :, D:E], 1.0).then_inc(ones_ready, 1)
                ring["keys"].taken(pool)
                for b in range(B):
                    pool.tensor_tensor(k_wide[:, b], spread(keys[:, b], 1, [P, H, G]),
                                       spread(t["head_of"][:, :], 2, [P, H, G]), ALU.mult).then_inc(wide_ready, 1)
                for b in range(B):
                    pool.tensor_tensor(x_bias[:, half(b)], x[:, half(b)], spread(rows["bo"], 1, [P, HT, P]),
                                       ALU.add).then_inc(x_bias_ready, 1)
                for n, units in enumerate(EM_LOADS):
                    pool.wait_ge(high_ready, n + 1)
                    low_part(pool, t["em_up_low"][:, units], t["em_up"][:, units],
                             t["em_up_high"][:, units]).then_inc(core.split_ready, 1)

            @block.vector
            def _(dve):
                step = core.steps(dve, "dve")
                core.wait_loaded(dve, "ca")
                s = ring["keys"]
                s.ready(dve)
                dve.tensor_scalar(keys[:, :, :].rearrange("p b g -> p (b g)"), s.ps[:, 0:B * G], bias["bk"],
                                  float(D) ** -0.5, ALU.add, ALU.mult).then_inc(s.drained, 1)
                s = ring["values"]
                s.ready(dve)
                for b in range(B):
                    ins = dve.tensor_tensor(v_one[:, b, :, 0:D],
                                            s.ps[0:G, b * P:(b + 1) * P].rearrange("p (h d) -> p h d", h=H),
                                            rows["bv"][0:G].rearrange("p (h d) -> p h d", h=H), ALU.add)
                    if b == 0:
                        step.mark(ins)
                    else:
                        ins.then_inc(s.drained, 1)

                def soften(g):
                    k = g % 2
                    if g >= 2:
                        ring[f"t3_{g - 2}"].ready(dve)
                    for n, (lo, hi) in enumerate(PARTS):
                        s = ring[f"s{n}_{g}"]
                        s.ready(dve)
                        dve.tensor_scalar(prob[:, k, lo:hi].rearrange("p h g -> p (h g)"), s.ps[:, 0:(hi - lo) * G],
                                          -CLAMP, CLAMP, ALU.max, ALU.min).then_inc(s.drained, 1)
                    for n in range(len(PARTS)):
                        ring[f"s{n}_{g}"].taken(dve)
                    step(dve.tensor_reduce(most[:, k], prob[:, k], AX.X, ALU.max))
                    dve.tensor_tensor(prob[:, k], prob[:, k], spread(most[:, k], 2, [P, H, G]),
                                      ALU.subtract).then_inc(shifted, 1)

                def divide(g):
                    k = g % 2
                    s = ring[f"o_{g}"]
                    s.ready(dve)
                    if g >= 2:
                        ring[f"yT_{g - 2}"].ready(dve)
                    num = s.ps[:, 0:H * E].rearrange("p (h e) -> p h e", e=E)
                    step(dve.reciprocal(den[:, k], num[:, :, D]))
                    dve.tensor_tensor(y[:, k].rearrange("p (h d) -> p h d", h=H), num[:, :, 0:D],
                                      spread(den[:, k], 2, [P, H, D]), ALU.mult).then_inc(s.drained, 1)

                def add(g):
                    s = ring[f"w_{g}"]
                    s.ready(dve)
                    dve.tensor_tensor(res[:, g], s.ps[:, 0:P], x_bias[:, g], ALU.add).then_inc(s.drained, 1)
                    if g % HT == HT - 1:
                        s.taken(dve)
                        hb = half(g // HT)
                        core.norm.dve(dve, step, res[:, hb], out[:, hb])

                def split(n):
                    core.wait_loaded(dve, f"em_{n}")
                    dve.tensor_copy(t["em_up_high"][:, EM_LOADS[n]], t["em_up"][:, EM_LOADS[n]]
                                    ).then_inc(high_ready, 1)

                dve.wait_ge(x_bias_ready, B)
                soften(0)
                soften(1)
                for g in range(NT):
                    if g + 2 < NT:
                        soften(g + 2)
                    divide(g)
                    if g:
                        add(g - 1)
                    if 2 <= g < 2 + len(EM_LOADS):
                        split(g - 2)
                add(NT - 1)
                step.wait()
                core.keep("dve", step)



HE = 256
NU = NE + 2
EM_UNITS = 6
EM_LOADS = [slice(e, e + EM_UNITS) for e in range(0, NU, EM_UNITS)]


def expert_mlp(core, x, out):
    nc = core.nc
    t = core.tiles
    with ExitStack() as ctx:
        def sb(name, shape, dt=F32):
            return core.tile("em_" + name, shape, dt, ctx)

        def sem(name):
            return ctx.enter_context(nc.semaphore("em_" + name))

        ident = t["ident"]
        rows = {n: t["rows"][:, a:b] for n, (a, b) in core.rows.items()}
        b_gate = t["cols"][:, core.cols["b1"][0]:core.cols["bs1"][1]]
        b_up = t["cols"][:, core.cols["b11"][0]:core.cols["bs11"][1]]
        xT = sb("xT", [P, NT, P])
        logit = sb("logit", [P, NT, NE])
        best = sb("best", [P, NT, 8])
        chosen = sb("chosen", [P, NT, NE])
        gate = sb("gate", [P, NT, NU])
        total = sb("total", [P, NT])
        gateT = sb("gateT", [NE, NT, P])
        acc = sb("acc", [P, NT, P])
        NS = 4
        silu = sb("silu", [P, NS, HT, P])
        x_high, x_low = sb("x_high", [P, NT, P], F32R), sb("x_low", [P, NT, P], F32R)
        hidden = sb("hidden", [P, 2, 2, HT, P])
        gated = sb("gated", [P, 2, HT, P])

        units = [(b, e) for b in range(B) for e in range(NU)]
        N = len(units)
        plan = []
        for b in range(B):
            plan += [f"xT{b}", f"logit{b}"]
        def up_banks(n):
            return [f"a0_{n}", f"u0_{n}", f"a1_{n}", f"u1_{n}"] if n < N else []

        plan += up_banks(0) + up_banks(1)
        plan += [f"gateT{b}" for b in range(B)] + [f"b2{b}" for b in range(B)]
        for n in range(N):
            plan += up_banks(n + 2) + [f"y_{n}"]
        ring = core.ring.plan(plan, range(BANKS))

        shifted, exps = sem("shifted"), sem("exps")
        gate_ready = sem("gate_ready")
        x_bias_ready = sem("x_bias_ready")
        ones_ready = sem("ones_ready")
        x_split = sem("x_split")
        gated_ready = sem("gated_ready")
        added = sem("added")

        def half(b):
            return slice(HT * b, HT * b + HT)

        with nc.Block() as block:
            @block.sync
            def _(sp):
                core.issue_loads(sp)

            @block.tensor
            def _(pe):
                core.wait_loaded(pe, "em")
                for b in range(B):
                    s = ring[f"xT{b}"]
                    s.claim(pe)
                    for i in range(HT):
                        ins = pe.transpose(s.ps[:, i * P:(i + 1) * P], x[:, HT * b + i], ident[:, :])
                    ins.then_inc(s.filled, 1)
                    s.taken(pe)
                    s = ring[f"logit{b}"]
                    s.claim(pe)
                    for i in range(HT):
                        ins = pe.matmul(s.ps[:, i * NE:(i + 1) * NE], xT[:, HT * b + i], t["em_wg"][:, :],
                                        start=True, stop=True, skip_group_check=True)
                    ins.then_inc(s.filled, 1)

                def up(n):
                    b, e = units[n]
                    if n < NU and n % EM_UNITS == 0:
                        core.wait_loaded(pe, f"em_{n // EM_UNITS}")
                        pe.wait_ge(core.split_ready, n // EM_UNITS + 1)
                    for j in range(2):
                        for name, at in ((f"a{j}_{n}", 0), (f"u{j}_{n}", HE)):
                            s = ring[name]
                            s.claim(pe)
                            cols = slice(at + j * P, at + (j + 1) * P)
                            three_passes(pe, s.ps[:, :], (t["em_up_high"][:, e, cols], t["em_up_low"][:, e, cols]),
                                         (x_high[:, half(b)], x_low[:, half(b)]), True, True).then_inc(s.filled, 1)

                def down(n):
                    e = units[n][1]
                    s = ring[f"y_{n}"]
                    s.claim(pe)
                    for j in range(2):
                        ring[f"u{j}_{n}"].taken(pe)
                    for i in range(HT):
                        for j in range(2):
                            ins = pe.matmul(s.ps[:, i * P:(i + 1) * P], hidden[:, n % 2, j, i],
                                            t["em_down"][:, e, j], start=(j == 0), stop=(j == 1),
                                            skip_group_check=True)
                    ins.then_inc(s.filled, 1)

                pe.wait_ge(x_split, B)
                up(0)
                up(1)
                for b in range(B):
                    s = ring[f"gateT{b}"]
                    s.claim(pe)
                    pe.wait_ge(gate_ready, 1)
                    for i in range(HT):
                        ins = pe.transpose(s.ps[0:NE, i * P:(i + 1) * P], gate[:, HT * b + i, 0:NE], ident[:, :])
                    ins.then_inc(s.filled, 1)
                for b in range(B):
                    ring[f"gateT{b}"].taken(pe)
                    s = ring[f"b2{b}"]
                    s.claim(pe)
                    for i in range(HT):
                        ins = pe.matmul(s.ps[:, i * P:(i + 1) * P], gateT[:, HT * b + i], t["em_b2"][:, :],
                                        start=True, stop=True, skip_group_check=True)
                    ins.then_inc(s.filled, 1)
                for n in range(N):
                    if n + 2 < N:
                        up(n + 2)
                    down(n)

            @block.scalar
            def _(act):
                step = core.steps(act, "act")
                load_exp_and_log(act)
                for b in range(B):
                    s = ring[f"xT{b}"]
                    s.ready(act)
                    act.copy(xT[:, half(b)], s.ps[:, :]).then_inc(s.drained, 1)
                act.wait_ge(shifted, 1)
                act.activation(gate[:, :, 0:NE], gate[:, :, 0:NE], ACT.Exp).then_inc(exps, 1)

                def weigh(n):
                    b, e = units[n]
                    s = ring[f"y_{n}"]
                    s.ready(act)
                    if n == 0:
                        act.wait_ge(ones_ready, 1)
                        act.wait_ge(gate_ready, 1)
                    if n >= 2:
                        act.wait_ge(added, n - 1)
                    for i in range(HT):
                        g = HT * b + i
                        act.activation(gated[:, n % 2, i], s.ps[:, i * P:(i + 1) * P], ACT.Copy,
                                       scale=gate[:, g, e:e + 1]).then_inc(gated_ready if i < HT - 1 else s.drained, 1)

                for n, (b, e) in enumerate(units):
                    if n == 1:
                        for c in range(B):
                            s = ring[f"gateT{c}"]
                            s.ready(act)
                            act.copy(gateT[:, half(c)], s.ps[0:NE, :]).then_inc(s.drained, 1)
                    for j in range(2):
                        m = 2 * n + j
                        if m >= NS:
                            old = m - NS
                            ring[f"u{old % 2}_{old // 2}"].taken(act)
                        s = ring[f"a{j}_{n}"]
                        s.ready(act)
                        act.activation(silu[:, m % NS], s.ps[:, :].rearrange("p (i t) -> p i t", i=HT), ACT.Silu,
                                       bias=b_gate[:, 2 * e + j:2 * e + j + 1]).then_inc(s.drained, 1)
                    if n >= 2:
                        weigh(n - 2)
                    if n == NU + 4:
                        load_exp_and_log(act)
                        core.norm.act(act, step)
                weigh(N - 2)
                weigh(N - 1)
                load_exp_and_log(act)
                core.norm.act(act, step)
                core.keep("act", step)

            @block.gpsimd
            def _(pool):
                pool.memset(gate[:, :, NE:NU], 1.0).then_inc(ones_ready, 1)
                for b in range(B):
                    pool.tensor_tensor(acc[:, half(b)], x[:, half(b)], spread(rows["bs2"], 1, [P, HT, P]),
                                       ALU.add).then_inc(x_bias_ready, 1)
                for b in range(B):
                    ring[f"b2{b}"].taken(pool)
                for n, (b, _) in enumerate(units):
                    pool.wait_ge(gated_ready, (HT - 1) * (n + 1))
                    ring[f"y_{n}"].taken(pool)
                    pool.tensor_tensor(acc[:, half(b)], acc[:, half(b)], gated[:, n % 2], ALU.add).then_inc(added, 1)
                    if n + 1 < N:
                        pool.wait_ge(added, n + 1)

            @block.vector
            def _(dve):
                step = core.steps(dve, "dve")
                core.wait_loaded(dve, "em")
                for b in range(B):
                    ring[f"xT{b}"].taken(dve)
                    step(dve.tensor_copy(x_high[:, half(b)], xT[:, half(b)]))
                    low_part(dve, x_low[:, half(b)], xT[:, half(b)], x_high[:, half(b)]).then_inc(x_split, 1)
                cube = [P, NT, NE]
                gt = gate[:, :, 0:NE]
                for b in range(B):
                    s = ring[f"logit{b}"]
                    s.ready(dve)
                    dve.tensor_copy(logit[:, half(b)], s.ps[:, 0:HT * NE].rearrange("p (i e) -> p i e", i=HT)
                                    ).then_inc(s.drained, 1)
                for b in range(B):
                    ring[f"logit{b}"].taken(dve)
                for g in range(NT):
                    step.mark(dve.max(best[:, g], logit[:, g]))
                step.wait()
                dve.tensor_tensor(gt, logit[:, :], spread(best[:, :, 0], 2, cube), ALU.subtract).then_inc(shifted, 1)
                step(dve.memset(best[:, :, 2:8], SELECTED))
                for g in range(NT):
                    step.mark(dve.match_replace(chosen[:, g], best[:, g], logit[:, g], SELECTED))
                dve.wait_ge(exps, 1)
                step.wait()
                step(dve.scalar_tensor_tensor(gt, chosen[:, :], SELECTED, gt, ALU.is_equal, ALU.mult))
                step(dve.tensor_reduce(total[:, :], gt, AX.X, ALU.add))
                step(dve.reciprocal(total[:, :], total[:, :]))
                dve.tensor_tensor(gt, gt, spread(total[:, :], 2, cube), ALU.mult).then_inc(gate_ready, 1)

                def lift(n):
                    e = units[n][1]
                    if n >= 2:
                        ring[f"y_{n - 2}"].ready(dve)
                    for j in range(2):
                        m = 2 * n + j
                        ring[f"a{j}_{n}"].taken(dve)
                        s = ring[f"u{j}_{n}"]
                        s.ready(dve)
                        dve.scalar_tensor_tensor(hidden[:, n % 2, j].rearrange("p i t -> p (i t)"), s.ps[:, :], b_up[:, 2 * e + j:2 * e + j + 1],
                                                 silu[:, m % NS].rearrange("p i t -> p (i t)"), ALU.add,
                                                 ALU.mult).then_inc(s.drained, 1)

                lift(0)
                dve.wait_ge(x_bias_ready, B)
                for b in range(B):
                    s = ring[f"b2{b}"]
                    s.ready(dve)
                    dve.tensor_tensor(acc[:, half(b)], s.ps[:, :].rearrange("p (i c) -> p i c", i=HT),
                                      acc[:, half(b)], ALU.add).then_inc(s.drained, 1)
                for n in range(1, N):
                    lift(n)
                    if n == NU + 4:
                        dve.wait_ge(added, NU)
                        core.norm.dve(dve, step, acc[:, half(0)], out[:, half(0)])
                dve.wait_ge(added, N)
                core.norm.dve(dve, step, acc[:, half(1)], out[:, half(1)])
                step.wait()
                core.keep("dve", step)


LAYERS = [linear_attention, cross_attention_ssm, expert_attention, gated_attention, cross_attention, expert_mlp]



ROWS = [("mod_gate", "L0_xattn_mod_gate"), ("g_in", "L0_xattn_g_norm_in"), ("b_in", "L0_xattn_b_norm_in"),
        ("d_skip", "L0_xattn_D_skip"), ("g_ffn", "L0_xattn_g_ffn"), ("b_ffn", "L0_xattn_b_ffn"),
        ("xa_b2", "L0_xattn_b2"), ("g_out", "L0_xattn_g_norm_out"), ("b_out", "L0_xattn_b_norm_out"),
        ("gates", "L0_ffn_gates"), ("gamma", "L1_attn_gamma"), ("beta", "L1_attn_beta"),
        ("bv", "L1_xattn_bv"), ("bo", "L1_xattn_bo"), ("bs2", "L1_ffn_bs2")]
COLS = [("xa_b1", "L0_xattn_b1"), ("wa_b", "L1_attn_Wa_b"), ("bq", "L1_xattn_bq"), ("bk", "L1_xattn_bk"),
        ("b1", "L1_ffn_b1"), ("bs1", "L1_ffn_bs1"), ("b11", "L1_ffn_b11"), ("bs11", "L1_ffn_bs11")]
ROW_SIZE = {"mod_gate": 1, "gates": 16}
COL_SIZE = {"xa_b1": 4, "wa_b": 4, "b1": 32, "b11": 32, "bs1": 4, "bs11": 4}


def places(names, size, default):
    at, out = 0, {}
    for n, _ in names:
        out[n] = (at, at + size.get(n, default))
        at = out[n][1]
    return out


def program(nc, io, out):
    with ExitStack() as ctx:
        core = Core(nc, ctx, io)
        core.norm = Norm(core)
        core.rows, core.cols = places(ROWS, ROW_SIZE, P), places(COLS, COL_SIZE, 1)
        x = [core.tile(f"x{n}", [P, NT, P]) for n in range(2)]
        core.experts = ctx.enter_context(ExitStack())
        core.early = ctx.enter_context(ExitStack())
        load_all(core, x[0])
        cur = 0
        for layer in LAYERS:
            layer(core, x[cur], x[1 - cur])
            cur = 1 - cur
            if layer is linear_attention:
                load_waves(core)
            if layer is cross_attention_ssm:
                core.early.close()
                core.late = ctx.enter_context(ExitStack())
                load_gated(core)
            if layer is gated_attention:
                core.late.close()
                core.experts.close()
                core.late = ctx.enter_context(ExitStack())
                load_last(core)
        stored = core.sem("stored")
        with nc.Block() as block:
            @block.sync
            def _(sp):
                for sem, n in core.loaded.values():
                    sp.wait_ge(sem, n)
                sp.dma_start(out.rearrange("b (i p) c -> p (b i) c", p=P), x[cur][:, :, :]).then_inc(stored, 16)
                sp.wait_ge(stored, 16)



def lay_out(inputs):
    f = {k: np.ascontiguousarray(v) for k, v in inputs.items()}
    p = np.arange(P)
    a = {
        "x": f["x"],
        "w_attn": f["L0_attn_w_attn"],
        "lin_w_proj": f["L0_attn_w_proj"],
        "ident": np.eye(P, dtype=np.float32),
        "causal": (p[None, :] >= p[:, None]).astype(np.float32),
        "head_of": (p[:, None] // 8 == np.arange(16)[None, :]).astype(np.float32),
        "head_block": (p[:, None] // 8 == np.arange(144)[None, :] // 9).astype(np.float32),
    }
    a["modes"] = np.concatenate([np.stack([f["L0_xattn_" + n].T for n in ("A_re", "A_im", "C_re", "C_im")], 1)] * 2, 0)
    a["log_dt"] = f["L0_xattn_log_dt"]
    top = (p < 64)[:, None]
    a["ssk_phase"] = np.where(top, [[0.25, 0.25, 0.5]], [[0.0, 0.5, 0.75]]).astype(np.float32)
    a["lag_a"] = np.tile(np.arange(LA, dtype=np.float32) * LB, (P, 1))
    a["lag_b"] = np.tile(np.arange(LB, dtype=np.float32), (P, 1))
    w = np.pi * (2 * np.arange(T) + 1) / (2 * T)
    for name, at in (("lag", np.arange(T)), ("half", np.arange(T) + 0.5)):
        a["cos_" + name] = np.cos(np.outer(at, w)).astype(np.float32)
        a["sin_" + name] = np.sin(np.outer(at, w)).astype(np.float32)
    a["rows"] = np.concatenate([f[key].reshape(-1) for _, key in ROWS])
    a["cols"] = np.concatenate([f[key].reshape(-1, P).T for _, key in COLS], 1)
    a["xa_wq"], a["xa_wk"], a["xa_wv"] = (f["L0_xattn_W" + n] for n in "qkv")
    a["ctxT"] = f["ctx_768"].transpose(2, 0, 1)
    a["head4_of"] = ((p[:, None] // 32 == np.arange(4)[None, :]) / np.sqrt(32.0)).astype(np.float32)
    a["xa_wfilm"] = np.concatenate([f["L0_xattn_W_film_in"], f["L0_xattn_W_film_out"]], 1)
    a["film_bias"] = np.concatenate([f["L0_xattn_b_film_in"], f["L0_xattn_b_film_out"]])[None, :]
    a["xa_w1"], a["xa_w2"] = f["L0_xattn_W1"], f["L0_xattn_W2"]
    a["mask_ctx"] = f["mask_BxS2_bf1"].view(np.uint8)
    a["mask_text"] = f["mask_BxS_bf1"].view(np.uint8).reshape(NT, P).T
    e = np.arange(48)[:, None, None] % 16
    a["expert_row"] = np.broadcast_to(np.where(e == np.arange(16)[None, :, None], 0x3F80, 0), (48, 16, P)).astype(np.uint16)
    a["expert_pair"] = np.where(e == 2 * np.arange(8)[None, :, None] + (p // 64), 0x3F80, 0).astype(np.uint16)
    a["sim"] = f["L0_ffn_sim_matrix"]
    a["causal_bias"] = np.where(p[None, :] <= p[:, None], 0, VERY_LOW).astype(np.float32)
    a["w_qkv"] = np.concatenate([f[f"L0_ffn_{n}_proj"] for n in "qkv"], 2).transpose(1, 0, 2)
    a["w_o"] = f["L0_ffn_o_proj"]
    a["ga_wqv"] = np.concatenate([f["L1_attn_Wq"], f["L1_attn_Wv"]], 0).T
    a["ga_wkk"] = np.concatenate([f["L1_attn_Wk"], f["L1_attn_Wk"]], 0).T
    a["ga_wa"] = f["L1_attn_Wa_w"].T
    a["restart"] = np.tile((np.arange(512) % BLK != 0).astype(np.float32), (P, 1))
    a["ga_qc"] = f["L1_attn_Qc"].transpose(1, 0, 2).reshape(64, 4, 128)
    a["ga_vcT"] = f["L1_attn_Vc"].transpose(2, 0, 1)
    a["ga_wo"] = f["L1_attn_Wo"].T
    a["causal_bits"] = np.broadcast_to((p[None, :] >= p[:, None])[:, None, :], (P, 4, P)).astype(np.uint32)
    a["ca_wk"], a["ca_wv"], a["ca_wq"], a["ca_wo"] = (f["L1_xattn_W" + n] for n in "kvqo")
    a["em_wg"], a["em_b2"] = f["L1_ffn_Wg"], f["L1_ffn_b2"]
    up = [np.concatenate([f["L1_ffn_" + n], f["L1_ffn_" + m].reshape(P, 2, HE).transpose(1, 0, 2)], 0)
          for n, m in (("W1", "Ws1"), ("W11", "Ws11"))]
    a["em_up"] = np.concatenate(up, 2).transpose(1, 0, 2)
    down = np.concatenate([f["L1_ffn_W2"], f["L1_ffn_Ws2"].reshape(2, HE, P)], 0)
    a["em_down"] = down.reshape(NU, 2, P, P).transpose(2, 0, 1, 3)
    return a


def kernel(**inputs):
    import concourse.bacc as _bacc
    from concourse.bass_utils import run_bass_kernel_spmd as _run

    nc = _bacc.Bacc("TRN2", target_bir_lowering=False, num_devices=1)
    arrays, io = {}, {}
    for name, a in lay_out(inputs).items():
        a = np.ascontiguousarray(a)
        arrays[f"in_{name}"] = a
        io[name] = nc.dram_tensor(f"in_{name}", a.shape, mybir.dt.from_np(a.dtype), kind="ExternalInput").ap()
    out = nc.dram_tensor("out_0_dram", (B, T, C), F32, kind="ExternalOutput").ap()
    program(nc, io, out)
    r = _run(nc, [arrays], core_ids=[0])
    return r.results[0]["out_0_dram"]
```
